# Optimizing a Trainium2 kernel written in Bass

```python
import numpy as np
import jax
import jax.numpy as jnp

def _softmax(x, axis=-1):
    return jax.nn.softmax(x, axis=axis)

def _gelu(x):
    return jax.nn.gelu(x, approximate=True)

def _silu(x):
    return jax.nn.silu(x)

def _sigmoid(x):
    return jax.nn.sigmoid(x)

def _layernorm(x, axis=-1, eps=1e-05):
    m = jnp.mean(x, axis=axis, keepdims=True)
    v = jnp.var(x, axis=axis, keepdims=True)
    return (x - m) / jnp.sqrt(v + eps)

def _scatter_add(tgt, idx, src, axis=0):
    return tgt.at[idx].add(src)

def _segment_sum(src, seg, n):
    return jax.ops.segment_sum(src, seg, n)
kernel_name = 'mk_gnn_preln_d1_gnn_r8_f48694'

def setup_inputs(seed: int=0):
    np.random.seed(seed)
    _w = jnp.asarray

    def _rec_inputs():
        import jax
        import jax.numpy as jnp
        _gk = jax.random.key(seed)
        x = -0.0003713 + 1 * jax.random.normal(jax.random.fold_in(_gk, 1), (12500, 128), jnp.float32)
        src = jax.random.randint(jax.random.fold_in(_gk, 2), (200000,), 0, 12500, jnp.int32)
        dst = jax.random.randint(jax.random.fold_in(_gk, 3), (200000,), 0, 12500, jnp.int32)
        _o = jnp.argsort(dst, stable=True)
        src = src[_o]
        dst = dst[_o]
        edge_attr_48 = -4.21973e-05 + 0.999841 * jax.random.normal(jax.random.fold_in(_gk, 11), (200000, 48), jnp.float32)
        return (x, src, dst, edge_attr_48)
    x, src, dst, edge_attr_48 = _rec_inputs()

    def _L0_gnn_setup():
        import jax, jax.numpy as jnp
        import numpy as np
        N_NODES = 12500
        N_EDGES = 200000
        NODE_DIM = 128
        EDGE_DIM = 48
        HID = 256
        OUT_DIM = 128
        IN_DIM = NODE_DIM + EDGE_DIM
        key = jax.random.key(seed)
        ks = jax.random.split(key, 10)

        def glorot(k, fan_in, fan_out):
            s = (6.0 / (fan_in + fan_out)) ** 0.5
            return jax.random.uniform(k, (fan_in, fan_out), jnp.float32, -s, s)
        return {'x': jax.random.normal(ks[0], (N_NODES, NODE_DIM), jnp.float32), 'edge_attr': jax.random.normal(ks[1], (N_EDGES, EDGE_DIM), jnp.float32), 'edge_index': jax.random.randint(ks[2], (2, N_EDGES), 0, N_NODES, jnp.int64), 'W1': glorot(ks[3], IN_DIM, HID), 'b1': jnp.zeros((HID,), jnp.float32), 'W2': glorot(ks[4], HID, HID), 'b2': jnp.zeros((HID,), jnp.float32), 'W3': glorot(ks[5], HID, OUT_DIM), 'b3': jnp.zeros((OUT_DIM,), jnp.float32)}
    _L0_gnn_all = _L0_gnn_setup()
    _L0_gnn_in = {k: v for k, v in _L0_gnn_all.items() if k in ('W1', 'b1', 'W2', 'b2', 'W3', 'b3')}
    del _L0_gnn_all
    return {'x': x, 'src': src, 'dst': dst, 'edge_attr_48': edge_attr_48, 'L0_gnn_W1': _L0_gnn_in['W1'], 'L0_gnn_b1': _L0_gnn_in['b1'], 'L0_gnn_W2': _L0_gnn_in['W2'], 'L0_gnn_b2': _L0_gnn_in['b2'], 'L0_gnn_W3': _L0_gnn_in['W3'], 'L0_gnn_b3': _L0_gnn_in['b3']}

def reference(x, src, dst, edge_attr_48, L0_gnn_W1, L0_gnn_b1, L0_gnn_W2, L0_gnn_b2, L0_gnn_W3, L0_gnn_b3):
    import jax
    import jax.numpy as jnp

    def _L0_gnn_ref(x, edge_attr, edge_index, W1, b1, W2, b2, W3, b3):
        import jax, jax.numpy as jnp
        import numpy as np
        N_NODES = 12500
        N_EDGES = 200000
        NODE_DIM = 128
        EDGE_DIM = 48
        HID = 256
        OUT_DIM = 128
        IN_DIM = NODE_DIM + EDGE_DIM
        r_idx = edge_index[1]
        agg_edge = jax.ops.segment_sum(edge_attr, r_idx, num_segments=N_NODES)
        collected = jnp.concatenate([x, agg_edge], axis=1)
        h = jax.nn.silu(collected @ W1 + b1)
        h = jax.nn.silu(h @ W2 + b2)
        delta_u = h @ W3 + b3
        new_u = x[:, -OUT_DIM:] + delta_u
        x_ = jnp.concatenate([x[:, :-OUT_DIM], new_u], axis=-1)
        return x_
    edge_index = jnp.stack([src, dst])
    h = jnp.maximum(_layernorm(x, axis=-1), 0.0)
    x = x + _L0_gnn_ref(h, edge_attr_48, edge_index, L0_gnn_W1, L0_gnn_b1, L0_gnn_W2, L0_gnn_b2, L0_gnn_W3, L0_gnn_b3)
    return x

_drawn_inputs = setup_inputs


def setup_inputs(seed=0):
    import zlib

    import numpy as np

    out = dict(_drawn_inputs(seed))
    spreads = {'L0_gnn_b1': (0.0, 0.273), 'L0_gnn_b2': (0.0, 0.1), 'L0_gnn_b3': (0.0, 0.1)}
    factors = {}
    for name, (base, spread) in spreads.items():
        noise = np.random.default_rng([zlib.crc32(name.encode()), seed]).standard_normal(out[name].shape)
        drawn = base * np.exp(spread * noise) if base else spread * noise
        out[name] = jnp.asarray(drawn.astype(out[name].dtype))
    for name, factor in factors.items():
        out[name] = (out[name] * factor).astype(out[name].dtype)
    return out
```

```python
from contextlib import ExitStack

import concourse.bass as bass
from concourse import mybir

ALU = mybir.AluOpType
ACT = mybir.ActivationFunctionType
AX = mybir.AxisListType
F32 = mybir.dt.float32
F32R = mybir.dt.float32r
I32 = mybir.dt.int32


def gnn_kernel(nc, x, dst, edge_attr, W1, b1, W2, b2, W3, b3, out):
    N, D = x.shape
    E, ED = edge_attr.shape
    HID = W1.shape[1]
    P = 128
    M = HID // P
    EPS = 1e-5

    PER = 4
    GROUP = P * PER
    NG = -(-E // GROUP)
    TAIL_P = (E - (NG - 1) * GROUP) // PER
    NPG = GROUP * N // E
    GPT = 14
    HALF = GPT // 2
    TILE = NPG * GPT
    TP = TILE // PER
    NT = -(-N // TILE)
    LAST_P = (N - (NT - 1) * TILE) // PER
    BANK = 512
    OVER = BANK - TILE
    WINDOW = 48
    EARLY = 3
    SLACK = EARLY * NPG
    ROWS = 4
    FULL_ROWS = NG // P
    LAST_G = NG - FULL_ROWS * P
    FAR = float(1 << 20)
    MAGIC = 1.5 * 2.0 ** 23
    assert N * GROUP == NPG * E and E % PER == 0 and N % PER == 0
    assert 2 * (WINDOW // 2) == WINDOW <= OVER and FULL_ROWS == ROWS - 1

    LOOP_FIRST, LOOP_END = 4, 24
    STEPS = NT + 2

    def groups_of(i, half):
        g0 = i * GPT + half * HALF if isinstance(i, int) else 0
        n = min(HALF, NG - g0)
        return n, min(n, NG - 1 - g0)

    def nodes_p(t):
        return LAST_P if isinstance(t, int) and t == NT - 1 else TP

    with ExitStack() as ctx:
        def sb(name, shape, dt=F32):
            return ctx.enter_context(nc.sbuf_tensor(name, shape, dt))

        def ps(name, shape, dt=F32):
            return ctx.enter_context(nc.psum_tensor(name, shape, dt))

        def sem(name):
            return ctx.enter_context(nc.semaphore(name))

        w1x = sb("w1x", [D, HID])
        w1e = sb("w1e", [2 * ED, HID])
        w2 = sb("w2", [P, M, HID])
        w3 = sb("w3", [P, M, D])
        b1c = sb("b1c", [P, M])
        b2c = sb("b2c", [P, M])
        b3r = sb("b3r", [P, D])
        ident = sb("ident", [P, P])
        ones = sb("ones", [P, P])
        window_i = sb("window_i", [P, WINDOW], I32)
        window = sb("window", [P, WINDOW])
        minus_half = sb("minus_half", [P, PER])
        eps = sb("eps", [P, PER])

        dst_rows = sb("dst_rows", [P, ROWS, GROUP], I32)
        rel_rows = sb("rel_rows", [P, ROWS, GROUP])
        first = sb("first", [P, ROWS], I32)
        even = sb("even", [P, ROWS], I32)
        lowest = sb("lowest", [P, ROWS])
        highest = sb("highest", [P, ROWS])
        centre_i = sb("centre_i", [P, ROWS], I32)
        g = {n: sb("g_" + n, [P, ROWS]) for n in (
            "base", "centre", "drift", "ok1", "ok2", "ok3", "ok4", "valid", "invalid", "basev",
            "tile", "tilet", "pair", "parity", "offset", "offset2", "shift")}
        rel = sb("rel", [P, NG, PER])
        offset_row = sb("offset_row", [1, ROWS * P], I32)
        any_invalid = sb("any_invalid", [1, 1], I32)

        raw = sb("raw", [P, 4, HALF, PER, ED])
        hilo = sb("hilo", [P, 4, HALF, PER, 2, ED], F32R)
        onehot = sb("onehot", [P, 4, HALF * PER, WINDOW], F32R)
        agg_carry = sb("agg_carry", [2 * ED, NT * TILE + OVER])

        gen_onehot = onehot[:, 2:4].rearrange("p s e w -> p (s e w)")[:, 0:PER * TILE].rearrange(
            "p (j n) -> p j n", j=PER)

        x_t = sb("x_t", [P, 2, PER, D])
        xb3 = sb("xb3", [P, 2, PER, D])
        stats = sb("stats", [P, PER, 6])
        meanvar = sb("meanvar", [P, 2, PER, 2])
        vareps = sb("vareps", [P, PER])
        rstd = sb("rstd", [P, 2, PER])
        xn = sb("xn", [P, 2, PER, D])
        resid = sb("resid", [P, 2, PER, D])
        hT = sb("hT", [D, 2, TILE])
        aggS = sb("aggS", [2 * ED, 2, TILE])
        h1 = sb("h1", [P, 2, M, TILE])
        h2 = sb("h2", [P, 2, M, TILE])
        out_t = sb("out_t", [P, 2, PER, D])

        gen_rel = h1[:, :, :, :].rearrange("p k m n -> p (k m n)")[:, 0:NG * PER].rearrange(
            "p (g j) -> p g j", j=PER)
        tile_cols = h2[:, 0, 0, :]
        tile_i = h2[:, 0, 1, :].bitcast(I32)
        gen_raw = sb("gen_raw", [P, PER, ED])
        gen_cols = sb("gen_cols", [P, PER])

        agg_ps = ps("agg_ps", [P, 2, BANK])
        z1 = ps("z1", [P, M, BANK])
        z2 = ps("z2", [P, M, BANK])
        z3 = ps("z3", [P, PER, D])
        tp = ps("tp", [P, BANK])

        s_const = sem("const_loaded")
        s_dst = sem("dst_loaded")
        s_pool_const = sem("pool_const")
        s_idx = sem("index_step")
        s_small = sem("small_ready")
        s_smallT = sem("small_transposed")
        s_off = sem("offsets_ready")
        s_relrow = sem("rel_rows_ready")
        s_relT = sem("rel_transposed")
        s_rel = sem("rel_ready")
        s_gen_rows = sem("general_rows")
        s_gen_relT = sem("general_transposed")
        s_gen_raw = sem("general_edges_loaded")
        s_gen_onehot = sem("general_onehot")
        s_gen_sum = sem("general_summed")
        s_gen_chain = sem("general_chain")
        s_carry0 = sem("carry_zeroed")
        s_edges = [sem(f"edges_loaded{k}") for k in range(4)]
        s_hi = sem("hi_ready")
        s_lo = sem("lo_ready")
        s_onehot = sem("onehot_ready")
        s_half = sem("half_summed")
        s_closed = sem("bank_closed")
        s_clear = sem("bank_clear")
        s_agg = sem("agg_ready")
        s_carried = sem("overhang_carried")
        s_x = [sem(f"x_loaded{k}") for k in range(2)]
        s_stats = sem("stats_ready")
        s_mv = sem("meanvar_ready")
        s_eps = sem("vareps_ready")
        s_rstd = sem("rstd_ready")
        s_xb3 = sem("xb3_ready")
        s_xn = sem("xn_ready")
        s_resid = sem("resid_ready")
        s_tp = sem("transposed")
        s_hT = sem("hT_ready")
        s_z1 = sem("z1_ready")
        s_h1 = sem("h1_ready")
        s_z2 = sem("z2_ready")
        s_h2 = sem("h2_ready")
        s_z3 = sem("z3_ready")
        s_out = sem("out_ready")
        s_stored = [sem(f"out_stored{k}") for k in range(2)]

        block = ctx.enter_context(nc.Block())

        def wait(eng, s, count):
            if isinstance(count, int) and count <= 0:
                return
            eng.wait_ge(s, count)

        def pipeline(eng, step):
            for i in range(LOOP_FIRST):
                step(i, i % 2)
            with eng.Fori(LOOP_FIRST, LOOP_END, 2) as i:
                for u in range(2):
                    step(i + u, u)
            for i in range(LOOP_END, STEPS):
                step(i, i % 2)

        def where_invalid(eng, engine_type, body):
            eng.wait_ge(s_off, 1)
            _, (flag,) = nc.values_load_multi_w_load_instructions(
                any_invalid[0:1, 0:1], engines=[engine_type], min_val=0, max_val=1,
                skip_runtime_bounds_check_because="it is computed as 0 or 1")
            with eng.If(flag):
                body()

        def has(i, lag, count):
            return not isinstance(i, int) or 0 <= i - lag < count

        def slot_turn(i, parity):
            return (i - parity) // 2 + 1 if isinstance(i, int) else (i - parity) // 2 + 1

        @block.sync
        def _(sp):
            rows = dst[0:FULL_ROWS * P * GROUP].rearrange("(c r e) -> r c e", r=P, e=GROUP)
            sp.dma_start(dst_rows[:, 0:FULL_ROWS, :], rows).then_inc(s_dst, 16)
            d0 = FULL_ROWS * P * GROUP
            sp.dma_start(dst_rows[0:LAST_G - 1, FULL_ROWS, :],
                         dst[d0:d0 + (LAST_G - 1) * GROUP].rearrange("(r e) -> r e", e=GROUP)).then_inc(s_dst, 16)
            n = TAIL_P * PER
            sp.dma_start(dst_rows[LAST_G - 1:LAST_G, FULL_ROWS, 0:n],
                         dst[E - n:E].rearrange("(r e) -> r e", r=1)).then_inc(s_dst, 16)
            sp.dma_start(dst_rows[LAST_G - 1:LAST_G, FULL_ROWS, n:GROUP],
                         dst[E - (GROUP - n):E].rearrange("(r e) -> r e", r=1)).then_inc(s_dst, 16)

            def load_edges(i, parity, half):
                n, full = groups_of(i, half)
                slot = 2 * parity + half
                wait(sp, s_lo, 2 * (i - 2) + half + 1)
                e0 = (i * GPT + half * HALF) * GROUP
                sp.dma_start(raw[:, slot, 0:full].rearrange("p g j d -> p g (j d)"),
                             edge_attr[bass.ds(e0, full * GROUP), :].rearrange(
                                 "(g p j) d -> p g (j d)", p=P, j=PER)).then_inc(s_edges[slot], 16)
                if full < n:
                    sp.dma_start(raw[0:TAIL_P, slot, full].rearrange("p j d -> p (j d)"),
                                 edge_attr[E - TAIL_P * PER:E, :].rearrange(
                                     "(p j) d -> p (j d)", j=PER)).then_inc(s_edges[slot], 16)

            def load_x(t, parity):
                wait(sp, s_resid, t - 1)
                wait(sp, s_xb3, t - 1)
                np_ = nodes_p(t)
                for a, b in ([(0, TP)] if np_ == TP else [(0, 96), (96, np_)]):
                    sp.dma_start(x_t[a:b, parity].rearrange("p q d -> p (q d)"),
                                 x[bass.ds(t * TILE + a * PER, (b - a) * PER), :].rearrange(
                                     "(p q) d -> p (q d)", q=PER)).then_inc(s_x[parity], 16)

            for half in range(2):
                load_edges(0, 0, half)
            load_x(0, 0)
            sp.dma_start(w1x[:, :], W1[0:D, :]).then_inc(s_const, 16)
            for k in range(2):
                sp.dma_start(w1e[k * ED:(k + 1) * ED, :], W1[D:D + ED, :]).then_inc(s_const, 16)
            sp.dma_start(w2[:, :, :], W2.rearrange("(m p) n -> p m n", p=P)).then_inc(s_const, 16)
            sp.dma_start(w3[:, :, :], W3.rearrange("(m p) n -> p m n", p=P)).then_inc(s_const, 16)
            sp.dma_start(b1c[:, :], b1.rearrange("(m p) -> p m", p=P), allow_slow_non_contiguous=True).then_inc(s_const, 16)
            sp.dma_start(b2c[:, :], b2.rearrange("(m p) -> p m", p=P), allow_slow_non_contiguous=True).then_inc(s_const, 16)
            sp.dma_start(b3r[:, :], b3.rearrange("(r n) -> r n", r=1).broadcast_to([P, D])).then_inc(s_const, 16)
            for half in range(2):
                load_edges(1, 1, half)

            def general_loads():
                def load(gr, rows):
                    sp.dma_start(gen_raw[0:rows].rearrange("p j d -> p (j d)"),
                                 edge_attr[bass.ds(gr * GROUP, rows * PER), :].rearrange(
                                     "(p j) d -> p (j d)", j=PER)).then_inc(s_gen_raw, 16)

                load(0, P)
                with sp.Fori(1, NG - 1) as gr:
                    sp.wait_ge(s_gen_sum, gr * NT)
                    load(gr, P)
                sp.wait_ge(s_gen_sum, (NG - 1) * NT)
                load(NG - 1, TAIL_P)

            where_invalid(sp, mybir.EngineType.SP, general_loads)

            def step(i, parity):
                if has(i, -1, NT):
                    load_x(i + 1, 1 - parity)
                if has(i, -2, NT):
                    for half in range(2):
                        load_edges(i + 2, parity, half)
                if has(i, 2, NT):
                    t = i - 2
                    sp.wait_ge(s_out, t + 1)
                    np_ = nodes_p(t)
                    for a, b in ([(0, TP)] if np_ == TP else [(0, 96), (96, np_)]):
                        sp.dma_start(out[bass.ds(t * TILE + a * PER, (b - a) * PER), :].rearrange(
                            "(p q) d -> p (q d)", q=PER),
                            out_t[a:b, parity].rearrange("p q d -> p (q d)")).then_inc(s_stored[parity], 16)

            pipeline(sp, step)
            sp.wait_ge(s_stored[0], 16 * (NT // 2))
            sp.wait_ge(s_stored[1], 16 * (NT // 2 + 1))

        CONSTS = 16 * 8

        @block.gpsimd
        def _(pool):
            pool.memset(ones[:, :], 1.0).then_inc(s_pool_const, 1)
            pool.iota(window_i[:, :], pattern=[[1, WINDOW]], base=0, channel_multiplier=0).then_inc(s_pool_const, 1)
            pool.iota(centre_i[:, :], pattern=[[NPG * P, ROWS]], base=0,
                      channel_multiplier=NPG).then_inc(s_pool_const, 1)
            pool.iota(tile_i[:, :], pattern=[[1, TILE]], base=0, channel_multiplier=0).then_inc(s_pool_const, 1)
            pool.memset(minus_half[:, :], -0.5).then_inc(s_pool_const, 1)
            pool.memset(eps[:, :], EPS).then_inc(s_pool_const, 1)
            pool.wait_ge(s_pool_const, 6)
            pool.affine_select(out=ident[:, :], in_=ones[:, :], compare_op=ALU.is_equal, fill=0.0, base=0,
                               pattern=[[-1, P]], channel_multiplier=1).then_inc(s_pool_const, 1)
            pool.memset(agg_carry[:, :], 0.0).then_inc(s_carry0, 1)

            def lo_part(i, parity, half):
                n, full = groups_of(i, half)
                slot = 2 * parity + half
                pool.wait_ge(s_hi, 2 * i + half + 1)
                for p, a, b in [(P, 0, full)] + ([(TAIL_P, full, n)] if full < n else []):
                    lo = pool.tensor_tensor(
                        hilo[0:p, slot, a:b, :, 1, :].rearrange("p g j d -> p (g j) d"),
                        raw[0:p, slot, a:b].rearrange("p g j d -> p (g j) d"),
                        hilo[0:p, slot, a:b, :, 0, :].rearrange("p g j d -> p (g j) d").bitcast(F32),
                        ALU.subtract)
                lo.then_inc(s_lo, 1)

            for half in range(2):
                lo_part(0, 0, half)
            pool.wait_ge(s_const, CONSTS)

            def step(i, parity):
                if has(i, 0, NT):
                    np_ = nodes_p(i)
                    wait(pool, s_x[parity], 16 * slot_turn(i, parity) + (16 if np_ != TP else 0))
                    wait(pool, s_resid, i - 1)
                    pool.tensor_tensor(xb3[0:np_, parity], x_t[0:np_, parity],
                                       b3r[0:np_, :].unsqueeze(1).broadcast_to([np_, PER, D]), ALU.add).then_inc(s_xb3, 1)
                if has(i, -1, NT):
                    lo_part(i + 1, 1 - parity, 0)
                if has(i, 0, NT):
                    pool.wait_ge(s_mv, i + 1)
                    wait(pool, s_xn, i - 1)
                    pool.tensor_tensor(vareps[0:np_, :], meanvar[0:np_, parity, :, 1], eps[0:np_, :],
                                       ALU.add).then_inc(s_eps, 1)
                    pool.wait_ge(s_eps, i + 1)
                    pool.tensor_tensor(rstd[0:np_, parity], vareps[0:np_, :], minus_half[0:np_, :],
                                       ALU.pow).then_inc(s_rstd, 1)
                if has(i, -1, NT):
                    lo_part(i + 1, 1 - parity, 1)

            pipeline(pool, step)

        @block.scalar
        def _(act):
            def hi_part(i, parity, half):
                n, full = groups_of(i, half)
                slot = 2 * parity + half
                wait(act, s_edges[slot], 16 * slot_turn(i, parity) + (16 if full < n else 0))
                wait(act, s_half, 2 * (i - 2) + half + 1)
                for p, a, b in [(P, 0, full)] + ([(TAIL_P, full, n)] if full < n else []):
                    hi = act.activation(hilo[0:p, slot, a:b, :, 0, :].rearrange("p g j d -> p (g j) d"),
                                        raw[0:p, slot, a:b].rearrange("p g j d -> p (g j) d"), ACT.Copy)
                hi.then_inc(s_hi, 1)

            for half in range(2):
                hi_part(0, 0, half)
            for c in range(ROWS):
                n = P if c < FULL_ROWS else LAST_G
                act.wait_ge(s_relT, c + 1)
                act.activation(rel[:, c * P:c * P + n, :],
                               (z1 if c < 2 else z2)[:, c % 2, :].rearrange("p (j r) -> p r j", j=PER)[:, 0:n, :],
                               ACT.Copy).then_inc(s_rel, 1)
            act.wait_ge(s_const, CONSTS)

            def step(i, parity):
                if has(i, -1, NT):
                    hi_part(i + 1, 1 - parity, 0)
                if has(i, 1, NT):
                    t, np_ = i - 1, nodes_p(i - 1)
                    act.wait_ge(s_tp, t + 1)
                    wait(act, s_z1, M * (t - 1))
                    act.activation(hT[:, 1 - parity, 0:PER * np_].rearrange("d (p q) -> d q p", q=PER),
                                   tp[:, 0:PER * np_].rearrange("d (q p) -> d q p", q=PER),
                                   ACT.Relu).then_inc(s_hT, 1)
                if has(i, 2, NT):
                    t, n = i - 2, PER * nodes_p(i - 2)
                    for m in range(M):
                        act.wait_ge(s_z2, M * t + m + 1)
                        wait(act, s_z3, t - 1)
                        act.activation(h2[:, parity, m, 0:n], z2[:, m, 0:n], ACT.Silu,
                                       bias=b2c[:, m:m + 1]).then_inc(s_h2, 1)
                if has(i, -1, NT):
                    hi_part(i + 1, 1 - parity, 1)
                if has(i, 1, NT):
                    t, n = i - 1, PER * nodes_p(i - 1)
                    for m in range(M):
                        act.wait_ge(s_z1, M * t + m + 1)
                        wait(act, s_z2, M * (t - 1))
                        act.activation(h1[:, 1 - parity, m, 0:n], z1[:, m, 0:n], ACT.Silu,
                                       bias=b1c[:, m:m + 1]).then_inc(s_h1, 1)

            pipeline(act, step)

        @block.vector
        def _(dve):
            links = [0]

            def link(ins):
                links[0] += 1
                ins.then_inc(s_idx, 1)
                dve.wait_ge(s_idx, links[0])

            for k in range(2):
                dve.memset(agg_ps[0:2 * ED, k, :], 0.0).then_inc(s_clear, 1)
            for tile in (first, lowest, highest):
                last = dve.memset(tile[:, :], 0)
            link(last)
            dve.wait_ge(s_dst, 64)
            for r, c in ((P, slice(0, FULL_ROWS)), (LAST_G, slice(FULL_ROWS, ROWS))):
                dve.tensor_copy(first[0:r, c], dst_rows[0:r, c, 0])
                dve.tensor_reduce(lowest[0:r, c], dst_rows[0:r, c, :], AX.X, ALU.min)
                last = dve.tensor_reduce(highest[0:r, c], dst_rows[0:r, c, :], AX.X, ALU.max)
            link(last)
            dve.wait_ge(s_pool_const, 7)
            dve.tensor_copy(window[:, :], window_i[:, :])
            dve.tensor_copy(g["centre"][:, :], centre_i[:, :])
            link(dve.tensor_scalar(even[:, :], first[:, :], -2, None, ALU.bitwise_and))
            link(dve.tensor_copy(g["base"][:, :], even[:, :]))
            link(dve.tensor_tensor(g["drift"][:, :], g["base"][:, :], g["centre"][:, :], ALU.subtract))
            dve.tensor_scalar(g["ok1"][:, :], g["drift"][:, :], -float(SLACK), None, ALU.is_ge)
            dve.tensor_scalar(g["ok2"][:, :], g["drift"][:, :], float(SLACK), None, ALU.is_le)
            dve.tensor_tensor(g["ok3"][:, :], lowest[:, :], g["base"][:, :], ALU.is_ge)
            link(dve.tensor_tensor(g["ok4"][:, :], highest[:, :], g["base"][:, :], ALU.subtract))
            link(dve.tensor_scalar(g["ok4"][:, :], g["ok4"][:, :], float(WINDOW - 1), None, ALU.is_le))
            link(dve.tensor_tensor(g["ok1"][:, :], g["ok1"][:, :], g["ok2"][:, :], ALU.mult))
            link(dve.tensor_tensor(g["ok3"][:, :], g["ok3"][:, :], g["ok4"][:, :], ALU.mult))
            link(dve.tensor_scalar(g["ok2"][:, :], g["base"][:, :], 0.0, None, ALU.is_ge))
            link(dve.tensor_tensor(g["ok3"][:, :], g["ok3"][:, :], g["ok2"][:, :], ALU.mult))
            link(dve.tensor_tensor(g["valid"][:, :], g["ok1"][:, :], g["ok3"][:, :], ALU.mult))
            link(dve.tensor_scalar(g["invalid"][:, :], g["valid"][:, :], -1.0, 1.0, ALU.mult, ALU.add))
            link(dve.scalar_tensor_tensor(g["shift"][:, :], g["invalid"][:, :], FAR, g["base"][:, :],
                                          ALU.mult, ALU.add))
            for c in range(ROWS):
                r = P if c < FULL_ROWS else LAST_G
                dve.tensor_scalar(rel_rows[0:r, c, :], dst_rows[0:r, c, :], g["shift"][0:r, c:c + 1], None,
                                  ALU.subtract).then_inc(s_relrow, 1)
            link(dve.tensor_tensor(g["basev"][:, :], g["drift"][:, :], g["valid"][:, :], ALU.mult))
            link(dve.tensor_tensor(g["basev"][:, :], g["basev"][:, :], g["centre"][:, :], ALU.add))
            link(dve.tensor_scalar(g["tilet"][:, :], g["basev"][:, :], 0.5 - TILE / 2, 1.0 / TILE, ALU.add, ALU.mult))
            link(dve.tensor_scalar(g["tile"][:, :], g["tilet"][:, :], MAGIC, -MAGIC, ALU.add, ALU.add))
            link(dve.tensor_scalar(g["tilet"][:, :], g["tile"][:, :], 0.5, -0.25, ALU.mult, ALU.add))
            link(dve.tensor_scalar(g["pair"][:, :], g["tilet"][:, :], MAGIC, -MAGIC, ALU.add, ALU.add))
            link(dve.scalar_tensor_tensor(g["parity"][:, :], g["pair"][:, :], -2.0, g["tile"][:, :],
                                          ALU.mult, ALU.add))
            link(dve.scalar_tensor_tensor(g["offset"][:, :], g["tile"][:, :], -float(TILE), g["basev"][:, :],
                                          ALU.mult, ALU.add))
            dve.scalar_tensor_tensor(g["offset2"][:, :], g["parity"][:, :], float(BANK), g["offset"][:, :],
                                     ALU.mult, ALU.add).then_inc(s_small, 1)
            dve.wait_ge(s_smallT, 1)
            dve.tensor_copy(offset_row[:, :], z3[0:1, :, :].rearrange("p q d -> p (q d)"))
            dve.tensor_reduce(any_invalid[:, :], tp[0:1, :], AX.X, ALU.max).then_inc(s_off, 1)

            dve.wait_ge(s_rel, ROWS)

            def general_path():
                chain = [0]

                def step_of(ins):
                    chain[0] += 1
                    ins.then_inc(s_gen_chain, 1)
                    dve.wait_ge(s_gen_chain, chain[0])

                dve.wait_ge(s_relT, ROWS)
                step_of(dve.tensor_scalar(g["ok1"][:, :], g["valid"][:, :], FAR, None, ALU.mult))
                for c in range(ROWS):
                    r = P if c < FULL_ROWS else LAST_G
                    dve.tensor_scalar(rel_rows[0:r, c, :], dst_rows[0:r, c, :], g["ok1"][0:r, c:c + 1], None,
                                      ALU.add).then_inc(s_gen_rows, 1)
                dve.tensor_copy(tile_cols[:, :], tile_i[:, :])
                dve.wait_ge(s_gen_relT, ROWS)
                dve.wait_ge(s_carry0, 1)
                for c in range(ROWS):
                    r = P if c < FULL_ROWS else LAST_G
                    ins = dve.tensor_copy(
                        gen_rel[:, c * P:c * P + r, :],
                        (z1 if c < 2 else z2)[:, c % 2, :].rearrange("p (j r) -> p r j", j=PER)[:, 0:r, :])
                step_of(ins)
                before = chain[0]

                def group(gr):
                    dve.tensor_copy(gen_cols[:, :], gen_rel[:, bass.ds(gr, 1), :].rearrange(
                        "p g j -> p (g j)")).then_inc(s_gen_chain, 1)
                    with dve.Fori(0, NT) as n:
                        dve.wait_ge(s_gen_chain, gr * (2 * NT + 1) + 2 * n + 1 + before)
                        for j in range(PER):
                            ins = dve.tensor_scalar(gen_onehot[:, j, :], tile_cols[:, :], gen_cols[:, j:j + 1], None,
                                                    ALU.is_equal)
                        ins.then_inc(s_gen_onehot, 1)
                        dve.wait_ge(s_gen_sum, gr * NT + n + 1)
                        into = agg_carry[0:ED, bass.ds(n * TILE, TILE)]
                        dve.tensor_tensor(into, z3[0:ED, :, :].rearrange("p q d -> p (q d)")[:, 0:TILE], into,
                                          ALU.add).then_inc(s_gen_chain, 1)
                        dve.wait_ge(s_gen_onehot, gr * NT + n + 1)
                        dve.tensor_scalar(gen_cols[:, :], gen_cols[:, :], -float(TILE), None,
                                          ALU.add).then_inc(s_gen_chain, 1)
                    dve.wait_ge(s_gen_chain, gr * (2 * NT + 1) + 2 * NT + 1 + before)

                with dve.Fori(0, NG) as gr:
                    group(gr)

            where_invalid(dve, mybir.EngineType.DVE, general_path)

            def make_onehot(i, parity, half):
                n, _ = groups_of(i, half)
                slot = 2 * parity + half
                wait(dve, s_half, 2 * (i - 2) + half + 1)
                cols = rel[:, :, :].rearrange("p g j -> p (g j)")[
                    :, bass.ds((i * GPT + half * HALF) * PER, n * PER)]
                dve.tensor_tensor(onehot[:, slot, 0:n * PER, :],
                                  window[:, :].unsqueeze(1).broadcast_to([P, n * PER, WINDOW]),
                                  cols.unsqueeze(2).broadcast_to([P, n * PER, WINDOW]), ALU.is_equal).then_inc(s_onehot, 1)

            for half in range(2):
                make_onehot(0, 0, half)

            def step(i, parity):
                if has(i, -1, NT):
                    make_onehot(i + 1, 1 - parity, 0)
                if has(i, 0, NT):
                    np_ = nodes_p(i)
                    dve.wait_ge(s_x[parity], 16 * slot_turn(i, parity) + (16 if np_ != TP else 0))
                    wait(dve, s_rstd, i - 1)
                    for q in range(PER):
                        st = dve.bn_stats(stats[0:np_, q, :], x_t[0:np_, parity, q, :])
                    st.then_inc(s_stats, 1)
                    dve.wait_ge(s_stats, i + 1)
                if has(i, 1, NT):
                    t, n = i - 1, PER * nodes_p(i - 1)
                    if isinstance(t, int) and t == NT - 1:
                        dve.wait_ge(s_half, 2 * NT)
                    else:
                        dve.wait_ge(s_closed, t + 1)
                    dve.wait_ge(s_carry0, 1)
                    wait(dve, s_carried, t)
                    wait(dve, s_z1, M * (t - 1))
                    dve.tensor_tensor(aggS[:, 1 - parity, 0:n], agg_ps[0:2 * ED, 1 - parity, 0:n],
                                      agg_carry[:, bass.ds(t * TILE, n)], ALU.add).then_inc(s_agg, 1)
                    if has(i, 1, NT - 1):
                        over = agg_carry[:, bass.ds((t + 1) * TILE, OVER)]
                        dve.tensor_tensor(over, agg_ps[0:2 * ED, 1 - parity, TILE:BANK], over,
                                          ALU.add).then_inc(s_carried, 1)
                    if has(i, 1, NT - 2):
                        dve.wait_ge(s_agg, t + 1)
                        dve.wait_ge(s_carried, t + 1)
                        dve.memset(agg_ps[0:2 * ED, 1 - parity, :], 0.0).then_inc(s_clear, 1)
                if has(i, 0, NT):
                    for q in range(PER):
                        mv = dve.bn_aggr(meanvar[0:np_, parity, q, :], stats[0:np_, q, :])
                    mv.then_inc(s_mv, 1)
                if has(i, -1, NT):
                    make_onehot(i + 1, 1 - parity, 1)
                if has(i, 0, NT):
                    dve.wait_ge(s_rstd, i + 1)
                    wait(dve, s_tp, i - 1)
                    for q in range(PER):
                        ln = dve.tensor_scalar(xn[0:np_, parity, q, :], x_t[0:np_, parity, q, :],
                                               meanvar[0:np_, parity, q, 0:1], rstd[0:np_, parity, q:q + 1],
                                               ALU.subtract, ALU.mult)
                    ln.then_inc(s_xn, 1)
                if has(i, 2, NT):
                    t, tp_ = i - 2, nodes_p(i - 2)
                    dve.wait_ge(s_z3, t + 1)
                    dve.wait_ge(s_resid, t + 1)
                    wait(dve, s_stored[parity], 16 * (slot_turn(t, parity) - 1))
                    dve.tensor_tensor(out_t[0:tp_, parity], z3[0:tp_, :, :], resid[0:tp_, parity],
                                      ALU.add).then_inc(s_out, 1)
                if has(i, 0, NT):
                    dve.wait_ge(s_xn, i + 1)
                    dve.wait_ge(s_xb3, i + 1)
                    wait(dve, s_out, i - 1)
                    dve.scalar_tensor_tensor(resid[0:np_, parity].rearrange("p q d -> p (q d)"),
                                             xn[0:np_, parity].rearrange("p q d -> p (q d)"), 0.0,
                                             xb3[0:np_, parity].rearrange("p q d -> p (q d)"),
                                             ALU.max, ALU.add).then_inc(s_resid, 1)

            pipeline(dve, step)

        @block.tensor
        def _(pe):
            pe.wait_ge(s_pool_const, 7)
            pe.wait_ge(s_small, 1)
            for c in range(ROWS):
                pe.matmul(z3[0:1, c, :], g["offset2"][:, c:c + 1], ident[:, :], start=True, stop=True)
            n_groups = [P] * FULL_ROWS + [LAST_G]
            for c, r in enumerate(n_groups):
                small = pe.matmul(tp[0:1, c * P:(c + 1) * P], g["invalid"][0:r, c:c + 1], ident[0:r, :],
                                  start=True, stop=True)
            small.then_inc(s_smallT, 1)
            for c, r in enumerate(n_groups):
                pe.wait_ge(s_relrow, c + 1)
                dst_bank = (z1 if c < 2 else z2)[:, c % 2, :]
                for j in range(PER):
                    tr = pe.transpose(dst_bank[:, j * P:j * P + r],
                                      rel_rows[0:r, c, :].rearrange("r (p j) -> r j p", j=PER)[:, j, :],
                                      ident[0:r, 0:r])
                tr.then_inc(s_relT, 1)

            def general_path():
                for c, r in enumerate(n_groups):
                    pe.wait_ge(s_gen_rows, c + 1)
                    pe.wait_ge(s_rel, ROWS)
                    for j in range(PER):
                        tr = pe.transpose((z1 if c < 2 else z2)[:, c % 2, j * P:j * P + r],
                                          rel_rows[0:r, c, :].rearrange("r (p j) -> r j p", j=PER)[:, j, :],
                                          ident[0:r, 0:r])
                    tr.then_inc(s_gen_relT, 1)

                def group(gr, rows):
                    with pe.Fori(0, NT) as n:
                        pe.wait_ge(s_gen_raw, (gr + 1) * 16)
                        pe.wait_ge(s_gen_onehot, gr * NT + n + 1)
                        for j in range(PER):
                            mm = pe.matmul(z3[0:ED, :, :].rearrange("p q d -> p (q d)")[:, 0:TILE],
                                           gen_raw[0:rows, j, :], gen_onehot[0:rows, j, :].bitcast(F32),
                                           start=(j == 0), stop=(j == PER - 1))
                        mm.then_inc(s_gen_sum, 1)

                with pe.Fori(0, NG - 1) as gr:
                    group(gr, P)
                group(NG - 1, TAIL_P)

            where_invalid(pe, mybir.EngineType.PE, general_path)
            banks = agg_ps[:, :, :].rearrange("p k n -> p (k n)")

            def step(i, parity):
                groups = min(GPT, NG - i * GPT) if isinstance(i, int) else GPT
                if has(i, 0, NT):
                    _, offs = nc.values_load_multi_w_load_instructions(
                        offset_row[0:1, bass.ds(i * GPT, groups)], engines=[mybir.EngineType.PE],
                        min_val=0, max_val=2 * BANK - WINDOW, skip_runtime_bounds_check_because="valid groups lie within SLACK of their tile")

                def sum_groups(a, b):
                    if not has(i, 0, NT):
                        return
                    for k in range(a, min(b, groups)):
                        half = k // HALF
                        if k % HALF == 0:
                            pe.wait_ge(s_lo, 2 * i + half + 1)
                            pe.wait_ge(s_onehot, 2 * i + half + 1)
                        if k == 0:
                            pe.wait_ge(s_clear, 2)
                        if k == GPT - EARLY and has(i, -1, NT):
                            pe.wait_ge(s_clear, i + 2)
                        slot = 2 * parity + half
                        rows = TAIL_P if isinstance(i, int) and i * GPT + k == NG - 1 else P
                        for j in range(PER):
                            mm = pe.matmul(banks[0:2 * ED, bass.ds(offs[k], WINDOW)],
                                           hilo[0:rows, slot, k % HALF, j].rearrange("p h d -> p (h d)"),
                                           onehot[0:rows, slot, (k % HALF) * PER + j, :],
                                           start=False, stop=True, skip_group_check=True)
                        if k % HALF == HALF - 1 or k == groups - 1:
                            mm.then_inc(s_half, 1)
                        elif k == EARLY - 1 and has(i, 1, NT):
                            mm.then_inc(s_closed, 1)

                sum_groups(0, EARLY)
                if has(i, 1, NT):
                    t, np_ = i - 1, nodes_p(i - 1)
                    pe.wait_ge(s_xn, t + 1)
                    wait(pe, s_hT, t)
                    if isinstance(t, int) and t == 0:
                        pe.wait_ge(s_off, 1)
                    for q in range(PER):
                        tr = pe.transpose(tp[:, q * np_:(q + 1) * np_], xn[0:np_, 1 - parity, q, :],
                                          ident[0:np_, 0:np_])
                    tr.then_inc(s_tp, 1)
                if has(i, 2, NT):
                    t, n = i - 2, PER * nodes_p(i - 2)
                    for m in range(M):
                        wait(pe, s_h2, M * (t - 1) + m + 1)
                        for k in range(M):
                            pe.wait_ge(s_h1, M * t + k + 1)
                            mm = pe.matmul(z2[:, m, 0:n], w2[:, k, m * P:(m + 1) * P], h1[:, parity, k, 0:n],
                                           start=(k == 0), stop=(k == M - 1))
                        mm.then_inc(s_z2, 1)
                sum_groups(EARLY, HALF)
                if has(i, 1, NT):
                    t, n = i - 1, PER * nodes_p(i - 1)
                    pe.wait_ge(s_hT, t + 1)
                    for m in range(M):
                        wait(pe, s_h1, M * (t - 1) + m + 1)
                        if isinstance(t, int) and t == 0:
                            pe.wait_ge(s_rel, ROWS)
                            pe.wait_ge(s_const, CONSTS)
                        pe.matmul(z1[:, m, 0:n], w1x[:, m * P:(m + 1) * P], hT[:, 1 - parity, 0:n],
                                  start=True, stop=False)
                        pe.wait_ge(s_agg, t + 1)
                        pe.matmul(z1[:, m, 0:n], w1e[:, m * P:(m + 1) * P], aggS[:, 1 - parity, 0:n],
                                  start=False, stop=True).then_inc(s_z1, 1)
                sum_groups(HALF, GPT - EARLY)
                if has(i, 2, NT):
                    t, np_ = i - 2, nodes_p(i - 2)
                    wait(pe, s_out, t)
                    pe.wait_ge(s_h2, M * t + M)
                    for q in range(PER):
                        for k in range(M):
                            mm = pe.matmul(z3[0:np_, q, :],
                                           h2[:, parity, k, 0:PER * np_].rearrange("c (p q) -> c q p", q=PER)[:, q, :],
                                           w3[:, k, :], start=(k == 0), stop=(k == M - 1))
                    mm.then_inc(s_z3, 1)
                sum_groups(GPT - EARLY, GPT)

            pipeline(pe, step)


_INS = ["x", "dst", "edge_attr_48", "L0_gnn_W1", "L0_gnn_b1", "L0_gnn_W2", "L0_gnn_b2", "L0_gnn_W3", "L0_gnn_b3"]


def kernel(**inputs):
    import numpy as _np
    import concourse.bacc as _bacc
    from concourse import mybir as _mybir
    from concourse.bass_utils import run_bass_kernel_spmd as _run

    nc = _bacc.Bacc("TRN2", target_bir_lowering=False, num_devices=1)
    arrays, args = {}, []
    for name in _INS:
        a = _np.ascontiguousarray(inputs[name])
        arrays[f"in_{name}_dram"] = a
        args.append(nc.dram_tensor(f"in_{name}_dram", a.shape, _mybir.dt.from_np(a.dtype), kind="ExternalInput").ap())
    out = nc.dram_tensor("out_0_dram", inputs["x"].shape, _mybir.dt.float32, kind="ExternalOutput").ap()
    gnn_kernel(nc, *args, out)
    r = _run(nc, [arrays], core_ids=[0])
    return r.results[0]["out_0_dram"]
```

```python
from contextlib import ExitStack

import concourse.bass as bass
from concourse import mybir

ALU = mybir.AluOpType
ACT = mybir.ActivationFunctionType
AX = mybir.AxisListType
F32 = mybir.dt.float32
F32R = mybir.dt.float32r
I32 = mybir.dt.int32


def gnn_kernel(nc, x, dst, edge_attr, W1, b1, W2, b2, W3, b3, out):
    N, D = x.shape
    E, ED = edge_attr.shape
    HID = W1.shape[1]
    P = 128
    M = HID // P
    EPS = 1e-5

    PER = 4
    GROUP = P * PER
    NG = -(-E // GROUP)
    TAIL_P = (E - (NG - 1) * GROUP) // PER
    NPG = GROUP * N // E
    GPT = 14
    HALF = GPT // 2
    PARTS = ((0, 5), (5, 10), (10, GPT))
    NPARTS = len(PARTS)
    PART = 5
    TILE = NPG * GPT
    TP = TILE // PER
    NT = -(-N // TILE)
    LAST_P = (N - (NT - 1) * TILE) // PER
    BANK = 512
    OVER = BANK - TILE
    WINDOW = 42
    EARLY = 3
    SLACK = EARLY * NPG
    ROWS = 4
    FULL_ROWS = NG // P
    LAST_G = NG - FULL_ROWS * P
    FAR = float(1 << 20)
    PLACE_K = 96
    ROW2 = 64
    MAGIC = 1.5 * 2.0 ** 23
    assert N * GROUP == NPG * E and E % PER == 0 and N % PER == 0
    assert WINDOW <= OVER and 2 * ED * PART <= BANK and FULL_ROWS == ROWS - 1

    LOOP_FIRST, LOOP_END = 4, 24
    STEPS = NT + 2

    def groups_of(i, half):
        g0 = i * GPT + half * HALF if isinstance(i, int) else 0
        n = min(HALF, NG - g0)
        return n, min(n, NG - 1 - g0)

    def part_of(i, s):
        a, b = PARTS[s]
        return a, min(b, NG - i * GPT) if isinstance(i, int) else b

    def nodes_p(t):
        return LAST_P if isinstance(t, int) and t == NT - 1 else TP

    with ExitStack() as ctx:
        def sb(name, shape, dt=F32):
            return ctx.enter_context(nc.sbuf_tensor(name, shape, dt))

        def ps(name, shape, dt=F32):
            return ctx.enter_context(nc.psum_tensor(name, shape, dt))

        def sem(name):
            return ctx.enter_context(nc.semaphore(name))

        w1x_hi = sb("w1x_hi", [D, HID], F32R)
        w1x_lo = sb("w1x_lo", [D, HID], F32R)
        w1e_hi = sb("w1e_hi", [ROW2 + ED, HID], F32R)
        w1e_lo = sb("w1e_lo", [ED, HID], F32R)
        w2_hi = sb("w2_hi", [P, M, HID], F32R)
        w2_lo = sb("w2_lo", [P, M, HID], F32R)
        w3 = sb("w3", [P, M, D])
        b1c = sb("b1c", [P, M])
        b2c = sb("b2c", [P, M])
        B3_LO = 32
        b3raw = sb("b3raw", [B3_LO + 1, D])
        b3hilo = sb("b3hilo", [B3_LO + 1, PER, D], F32R)
        ones_r = sb("ones_r", [B3_LO + 1, TP], F32R)
        zeros = sb("zeros", [P, 1])
        ident = sb("ident", [P, P])
        window_i = sb("window_i", [P, WINDOW], I32)
        window = sb("window", [P, WINDOW])
        minus_half = sb("minus_half", [P, PER])
        eps = sb("eps", [P, PER])

        dst_rows = sb("dst_rows", [P, ROWS, GROUP], I32)
        rel_rows = sb("rel_rows", [P, ROWS, GROUP])
        lowest = sb("lowest", [P, ROWS])
        highest = sb("highest", [P, ROWS])
        centre_i = sb("centre_i", [P, ROWS], I32)
        g = {n: sb("g_" + n, [P, ROWS]) for n in (
            "base", "centre", "drift", "ok1", "ok2", "ok3", "ok4", "valid", "invalid",
            "tile", "tilet", "tile_half", "pair", "parity", "offset", "offset2", "offset3",
            "at_centre", "instead", "placed", "shift")}
        rel = sb("rel", [P, NG, PER])
        offset_row = sb("offset_row", [1, ROWS * P], I32)
        any_invalid = sb("any_invalid", [1, 1], I32)

        raw = sb("raw", [P, 4, HALF, PER, ED])
        hilo = sb("hilo", [P, 4, HALF, PER, 2, ED], F32R)
        onehot = sb("onehot", [P, 4, HALF * PER, WINDOW], F32R)
        staged = sb("staged", [PLACE_K, 2, PART, ED])
        agg_carry = sb("agg_carry", [ED, NT * TILE + OVER])

        gen_onehot = onehot[:, 2:4].rearrange("p s e w -> p (s e w)")[:, 0:PER * TILE].rearrange(
            "p (j n) -> p j n", j=PER)

        x_t = sb("x_t", [P, 2, PER, D])
        stats = sb("stats", [P, PER, 6])
        meanvar = sb("meanvar", [P, 2, PER, 2])
        vareps = sb("vareps", [P, PER])
        rstd = sb("rstd", [P, 2, PER])
        xn = sb("xn", [P, 2, PER, D])
        resid = sb("resid", [P, 2, PER, D])
        hT_hi = sb("hT_hi", [D, TILE], F32R)
        hT_lo = sb("hT_lo", [D, TILE], F32R)
        agg = sb("agg", [ED, TILE])
        agg_hilo = sb("agg_hilo", [ROW2 + ED, TILE], F32R)
        h = sb("h", [P, 2 * M, TILE])
        h1, h2 = h[:, 0:M], h[:, M:2 * M]
        h1_hi = sb("h1_hi", [P, M, TILE], F32R)
        h1_lo = sb("h1_lo", [P, M, TILE], F32R)
        ones = resid[:, 1, 0, :]
        b3hi = h1_hi[0:B3_LO + 1, 0, 0:D]
        out_t = sb("out_t", [P, 2, PER, D])
        load_w = out_t[:, :, :, :].rearrange("p k q d -> p (k q d)")
        w2_in = load_w[:, 0:M * HID].rearrange("p (m n) -> p m n", m=M)
        w1x_in = load_w[:, M * HID:(M + 1) * HID]
        w1e_in = load_w[0:ROW2 + ED, (M + 1) * HID:(M + 2) * HID]

        gen_rel = h[:, :, :].rearrange("p m n -> p (m n)")[:, 0:NG * PER].rearrange(
            "p (g j) -> p g j", j=PER)
        tables = xn[:, :, :, :].rearrange("p k q d -> p (k q d)")
        tile_cols = tables[:, 0:TILE]
        tile_i = tables[:, TILE:2 * TILE].bitcast(I32)
        gen_raw = resid[:, 0].rearrange("p q d -> p (q d)")[:, 0:PER * ED].rearrange("p (j d) -> p j d", j=PER)
        gen_cols = sb("gen_cols", [P, PER])

        agg_ps = ps("agg_ps", [P, 2, BANK])
        tp = ps("tp", [P, BANK])
        stage = ps("stage", [P, 2, BANK])
        z = ps("z", [P, M, BANK])
        z3 = ps("z3", [P, PER, D])
        row_banks = (z[:, 0, :], z[:, 1, :], z3[:, :, :].rearrange("p q d -> p (q d)"), tp[:, :])

        s_const = sem("const_loaded")
        s_dst = sem("dst_loaded")
        s_pool_const = sem("pool_const")
        s_idx = sem("index_step")
        s_small = sem("small_ready")
        s_smallT = sem("small_transposed")
        s_off = sem("offsets_ready")
        s_relrow = sem("rel_rows_ready")
        s_relT = sem("rel_transposed")
        s_rel = sem("rel_ready")
        s_gen_rows = sem("general_rows")
        s_gen_relT = sem("general_transposed")
        s_gen_raw = sem("general_edges_loaded")
        s_gen_onehot = sem("general_onehot")
        s_resummed = sem("first_part_resummed")
        s_gen_sum = sem("general_summed")
        s_gen_chain = sem("general_chain")
        s_carry0 = sem("carry_zeroed")
        s_edges = [sem(f"edges_loaded{k}") for k in range(4)]
        s_hi = sem("hi_ready")
        s_lo = sem("lo_ready")
        s_onehot = sem("onehot_ready")
        s_summed = sem("part_summed")
        s_staged = sem("part_staged")
        s_placed = sem("part_placed")
        s_closed = sem("bank_closed")
        s_clear = sem("bank_clear")
        s_agg = sem("agg_ready")
        s_agg_hi = sem("agg_hi_ready")
        s_agg_lo = sem("agg_lo_ready")
        s_w_hi = sem("weights_hi_ready")
        s_w_lo = sem("weights_lo_ready")
        s_carried = sem("overhang_carried")
        s_x = [sem(f"x_loaded{k}") for k in range(2)]
        s_stats = sem("stats_ready")
        s_mv = sem("meanvar_ready")
        s_eps = sem("vareps_ready")
        s_rstd = sem("rstd_ready")
        s_b3 = sem("b3_ready")
        s_xn = sem("xn_ready")
        s_resid = sem("resid_ready")
        s_tp = sem("transposed")
        s_hT = sem("hT_hi_ready")
        s_hT_lo = sem("hT_lo_ready")
        s_z1 = sem("z1_ready")
        s_h1 = sem("h1_ready")
        s_h1_hi = sem("h1_hi_ready")
        s_h1_lo = sem("h1_lo_ready")
        s_z2 = sem("z2_ready")
        s_h2 = sem("h2_ready")
        s_z3 = sem("z3_ready")
        s_out = sem("out_ready")
        s_stored = [sem(f"out_stored{k}") for k in range(2)]

        block = ctx.enter_context(nc.Block())

        def wait(eng, s, count):
            if isinstance(count, int) and count <= 0:
                return
            eng.wait_ge(s, count)

        def pipeline(eng, step):
            for i in range(LOOP_FIRST):
                step(i, i % 2)
            with eng.Fori(LOOP_FIRST, LOOP_END, 2) as i:
                for u in range(2):
                    step(i + u, u)
            for i in range(LOOP_END, STEPS):
                step(i, i % 2)

        def where_invalid(eng, engine_type, body):
            eng.wait_ge(s_off, 1)
            _, (flag,) = nc.values_load_multi_w_load_instructions(
                any_invalid[0:1, 0:1], engines=[engine_type], min_val=0, max_val=1,
                skip_runtime_bounds_check_because="it is computed as 0 or 1")
            with eng.If(flag):
                body()

        def has(i, lag, count):
            return not isinstance(i, int) or 0 <= i - lag < count

        def slot_turn(i, parity):
            return (i - parity) // 2 + 1

        @block.sync
        def _(sp):
            rows = dst[0:FULL_ROWS * P * GROUP].rearrange("(c r e) -> r c e", r=P, e=GROUP)
            sp.dma_start(dst_rows[:, 0:FULL_ROWS, :], rows).then_inc(s_dst, 16)
            d0 = FULL_ROWS * P * GROUP
            sp.dma_start(dst_rows[0:LAST_G - 1, FULL_ROWS, :],
                         dst[d0:d0 + (LAST_G - 1) * GROUP].rearrange("(r e) -> r e", e=GROUP)).then_inc(s_dst, 16)
            n = TAIL_P * PER
            sp.dma_start(dst_rows[LAST_G - 1:LAST_G, FULL_ROWS, 0:n],
                         dst[E - n:E].rearrange("(r e) -> r e", r=1)).then_inc(s_dst, 16)
            sp.dma_start(dst_rows[LAST_G - 1:LAST_G, FULL_ROWS, n:GROUP],
                         dst[E - (GROUP - n):E].rearrange("(r e) -> r e", r=1)).then_inc(s_dst, 16)

            def load_edges(i, parity, half):
                n, full = groups_of(i, half)
                slot = 2 * parity + half
                wait(sp, s_lo, 2 * (i - 2) + half + 1)
                e0 = (i * GPT + half * HALF) * GROUP
                sp.dma_start(raw[:, slot, 0:full].rearrange("p g j d -> p g (j d)"),
                             edge_attr[bass.ds(e0, full * GROUP), :].rearrange(
                                 "(g p j) d -> p g (j d)", p=P, j=PER)).then_inc(s_edges[slot], 16)
                if full < n:
                    sp.dma_start(raw[0:TAIL_P, slot, full].rearrange("p j d -> p (j d)"),
                                 edge_attr[E - TAIL_P * PER:E, :].rearrange(
                                     "(p j) d -> p (j d)", j=PER)).then_inc(s_edges[slot], 16)

            def load_x(t, parity):
                wait(sp, s_resid, t - 1)
                np_ = nodes_p(t)
                for a, b in ([(0, TP)] if np_ == TP else [(0, 96), (96, np_)]):
                    sp.dma_start(x_t[a:b, parity].rearrange("p q d -> p (q d)"),
                                 x[bass.ds(t * TILE + a * PER, (b - a) * PER), :].rearrange(
                                     "(p q) d -> p (q d)", q=PER)).then_inc(s_x[parity], 16)

            for half in range(2):
                load_edges(0, 0, half)
            load_x(0, 0)
            sp.dma_start(w2_in, W2.rearrange("(m p) n -> p m n", p=P)).then_inc(s_const, 16)
            sp.dma_start(w1x_in, W1[0:D, :]).then_inc(s_const, 16)
            for a in (0, ROW2):
                sp.dma_start(w1e_in[a:a + ED, :], W1[D:D + ED, :]).then_inc(s_const, 16)
            sp.dma_start(w3[:, :, :], W3.rearrange("(m p) n -> p m n", p=P)).then_inc(s_const, 16)
            sp.dma_start(b1c[:, :], b1.rearrange("(m p) -> p m", p=P), allow_slow_non_contiguous=True).then_inc(s_const, 16)
            sp.dma_start(b2c[:, :], b2.rearrange("(m p) -> p m", p=P), allow_slow_non_contiguous=True).then_inc(s_const, 16)
            for p in (0, B3_LO):
                sp.dma_start(b3raw[p:p + 1, :], b3.rearrange("(r n) -> r n", r=1)).then_inc(s_const, 16)
            for half in range(2):
                load_edges(1, 1, half)

            def general_loads():
                def load(gr, rows):
                    sp.dma_start(gen_raw[0:rows].rearrange("p j d -> p (j d)"),
                                 edge_attr[bass.ds(gr * GROUP, rows * PER), :].rearrange(
                                     "(p j) d -> p (j d)", j=PER)).then_inc(s_gen_raw, 16)

                load(0, P)
                with sp.Fori(1, NG - 1) as gr:
                    sp.wait_ge(s_gen_sum, gr * NT)
                    load(gr, P)
                sp.wait_ge(s_gen_sum, (NG - 1) * NT)
                load(NG - 1, TAIL_P)

            where_invalid(sp, mybir.EngineType.SP, general_loads)

            def step(i, parity):
                if has(i, -1, NT):
                    load_x(i + 1, 1 - parity)
                if has(i, -2, NT):
                    for half in range(2):
                        load_edges(i + 2, parity, half)
                if has(i, 2, NT):
                    t = i - 2
                    sp.wait_ge(s_out, t + 1)
                    np_ = nodes_p(t)
                    for a, b in ([(0, TP)] if np_ == TP else [(0, 96), (96, np_)]):
                        sp.dma_start(out[bass.ds(t * TILE + a * PER, (b - a) * PER), :].rearrange(
                            "(p q) d -> p (q d)", q=PER),
                            out_t[a:b, parity].rearrange("p q d -> p (q d)")).then_inc(s_stored[parity], 16)

            pipeline(sp, step)
            sp.wait_ge(s_stored[0], 16 * (NT // 2))
            sp.wait_ge(s_stored[1], 16 * (NT // 2 + 1))

        CONSTS = 16 * 9

        @block.gpsimd
        def _(pool):
            pool.memset(ones, 1.0).then_inc(s_pool_const, 1)
            pool.iota(window_i[:, :], pattern=[[1, WINDOW]], base=0, channel_multiplier=0).then_inc(s_pool_const, 1)
            pool.iota(centre_i[:, :], pattern=[[NPG * P, ROWS]], base=0,
                      channel_multiplier=NPG).then_inc(s_pool_const, 1)
            pool.iota(tile_i[:, :], pattern=[[1, TILE]], base=0, channel_multiplier=0).then_inc(s_pool_const, 1)
            pool.memset(minus_half[:, :], -0.5).then_inc(s_pool_const, 1)
            pool.memset(eps[:, :], EPS).then_inc(s_pool_const, 1)
            pool.memset(ones_r[:, :].bitcast(F32), 1.0).then_inc(s_pool_const, 1)
            pool.memset(b3hilo[:, :, :].bitcast(F32), 0.0).then_inc(s_pool_const, 1)
            pool.memset(agg_hilo[:, :].bitcast(F32), 0.0).then_inc(s_pool_const, 1)
            pool.memset(w1e_hi[:, :].bitcast(F32), 0.0).then_inc(s_pool_const, 1)
            pool.memset(zeros[:, :], 0.0).then_inc(s_pool_const, 1)
            pool.memset(staged[:, :, :, :], 0.0).then_inc(s_pool_const, 1)
            pool.wait_ge(s_pool_const, 12)
            pool.affine_select(out=ident[:, :], in_=ones, compare_op=ALU.is_equal, fill=0.0, base=0,
                               pattern=[[-1, P]], channel_multiplier=1).then_inc(s_pool_const, 1)
            pool.memset(agg_carry[:, :], 0.0).then_inc(s_carry0, 1)

            def lo_part(i, parity, half):
                n, full = groups_of(i, half)
                slot = 2 * parity + half
                pool.wait_ge(s_hi, 2 * i + half + 1)
                for p, a, b in [(P, 0, full)] + ([(TAIL_P, full, n)] if full < n else []):
                    lo = pool.tensor_tensor(
                        hilo[0:p, slot, a:b, :, 1, :].rearrange("p g j d -> p (g j) d"),
                        raw[0:p, slot, a:b].rearrange("p g j d -> p (g j) d"),
                        hilo[0:p, slot, a:b, :, 0, :].rearrange("p g j d -> p (g j) d").bitcast(F32),
                        ALU.subtract)
                lo.then_inc(s_lo, 1)

            for half in range(2):
                lo_part(0, 0, half)
            pool.wait_ge(s_w_hi, 4)
            pool.tensor_tensor(w2_lo[:, :, :].rearrange("p m n -> p (m n)"), w2_in.rearrange("p m n -> p (m n)"),
                               w2_hi[:, :, :].rearrange("p m n -> p (m n)").bitcast(F32),
                               ALU.subtract).then_inc(s_w_lo, 1)
            pool.tensor_tensor(w1x_lo[:, :], w1x_in, w1x_hi[:, :].bitcast(F32), ALU.subtract).then_inc(s_w_lo, 1)
            pool.tensor_tensor(w1e_lo[:, :], w1e_in[0:ED, :], w1e_hi[0:ED, :].bitcast(F32),
                               ALU.subtract).then_inc(s_w_lo, 1)

            def step(i, parity):
                if has(i, -1, NT):
                    for half in range(2):
                        lo_part(i + 1, 1 - parity, half)
                if has(i, 0, NT):
                    np_ = nodes_p(i)
                    pool.wait_ge(s_mv, i + 1)
                    wait(pool, s_xn, i - 1)
                    pool.tensor_tensor(vareps[0:np_, :], meanvar[0:np_, parity, :, 1], eps[0:np_, :],
                                       ALU.add).then_inc(s_eps, 1)
                    pool.wait_ge(s_eps, i + 1)
                    pool.tensor_tensor(rstd[0:np_, parity], vareps[0:np_, :], minus_half[0:np_, :],
                                       ALU.pow).then_inc(s_rstd, 1)
                if has(i, 1, NT):
                    t, n = i - 1, PER * nodes_p(i - 1)
                    for m in range(M):
                        pool.wait_ge(s_h1_hi, M * t + m + 1)
                        wait(pool, s_z2, M * t)
                        pool.tensor_tensor(h1_lo[:, m, 0:n], h1[:, m, 0:n], h1_hi[:, m, 0:n].bitcast(F32),
                                           ALU.subtract).then_inc(s_h1_lo, 1)

            pipeline(pool, step)

        @block.scalar
        def _(act):
            def hi_part(i, parity, half):
                n, full = groups_of(i, half)
                slot = 2 * parity + half
                wait(act, s_edges[slot], 16 * slot_turn(i, parity) + (16 if full < n else 0))
                wait(act, s_summed, NPARTS * (i - 2) + half + 2)
                for p, a, b in [(P, 0, full)] + ([(TAIL_P, full, n)] if full < n else []):
                    hi = act.activation(hilo[0:p, slot, a:b, :, 0, :].rearrange("p g j d -> p (g j) d"),
                                        raw[0:p, slot, a:b].rearrange("p g j d -> p (g j) d"), ACT.Copy)
                hi.then_inc(s_hi, 1)

            hi_part(0, 0, 0)
            for c in range(ROWS):
                n = P if c < FULL_ROWS else LAST_G
                act.wait_ge(s_relT, c + 1)
                act.activation(rel[:, c * P:c * P + n, :],
                               row_banks[c].rearrange("p (j r) -> p r j", j=PER)[:, 0:n, :],
                               ACT.Copy).then_inc(s_rel, 1)
                if c == 0:
                    hi_part(0, 0, 1)
            act.wait_ge(s_const, CONSTS)
            act.wait_ge(s_pool_const, 11)
            act.activation(w2_hi[:, :, :].rearrange("p m n -> p (m n)"), w2_in.rearrange("p m n -> p (m n)"),
                           ACT.Copy).then_inc(s_w_hi, 1)
            act.activation(w1x_hi[:, :], w1x_in, ACT.Copy).then_inc(s_w_hi, 1)
            for a in (0, ROW2):
                act.activation(w1e_hi[a:a + ED, :], w1e_in[a:a + ED, :], ACT.Copy).then_inc(s_w_hi, 1)
            for p in (0, B3_LO):
                act.activation(b3hi[p:p + 1, :], b3raw[p:p + 1, :], ACT.Copy).then_inc(s_b3, 1)
            act.activation(b3hilo[0:1], b3raw[0:1, :].unsqueeze(1).broadcast_to([1, PER, D]),
                           ACT.Copy).then_inc(s_b3, 1)

            def clear_bank(k):
                act.activation(agg_ps[0:ED, k, :], zeros[0:ED, :].broadcast_to([ED, BANK]),
                               ACT.Copy).then_inc(s_clear, 1)

            act.wait_ge(s_off, 1)
            for k in range(2):
                clear_bank(k)
            hi_part(1, 1, 0)

            def step(i, parity):
                if has(i, 1, NT):
                    t, np_ = i - 1, nodes_p(i - 1)
                    act.wait_ge(s_tp, t + 1)
                    wait(act, s_z1, M * t)
                    act.activation(hT_hi[:, 0:PER * np_].rearrange("d (p q) -> d q p", q=PER),
                                   tp[:, 0:PER * np_].rearrange("d (q p) -> d q p", q=PER),
                                   ACT.Relu).then_inc(s_hT, 1)
                if has(i, -1, NT):
                    hi_part(i + 1, 1 - parity, 1)
                if has(i, 2, NT):
                    t, n = i - 2, PER * nodes_p(i - 2)
                    for m in range(M):
                        act.wait_ge(s_z2, M * t + m + 1)
                        wait(act, s_z3, t)
                        act.activation(h2[:, m, 0:n], z[:, m, 0:n], ACT.Silu,
                                       bias=b2c[:, m:m + 1]).then_inc(s_h2, 1)
                if has(i, 1, NT):
                    t, n = i - 1, PER * nodes_p(i - 1)
                    act.wait_ge(s_agg, t + 1)
                    wait(act, s_z1, M * t)
                    act.activation(agg_hilo[0:ED, 0:n], agg[:, 0:n], ACT.Copy).then_inc(s_agg_hi, 1)
                    if has(i, 1, NT - 2):
                        act.wait_ge(s_carried, t + 1)
                        clear_bank(1 - parity)
                if has(i, -2, NT):
                    hi_part(i + 2, parity, 0)
                if has(i, 1, NT):
                    t, n = i - 1, PER * nodes_p(i - 1)
                    for m in range(M):
                        act.wait_ge(s_z1, M * t + m + 1)
                        wait(act, s_h1_lo, M * (t - 1) + m + 1)
                        act.activation(h1[:, m, 0:n], z[:, m, 0:n], ACT.Silu,
                                       bias=b1c[:, m:m + 1]).then_inc(s_h1, 1)
                        act.wait_ge(s_h1, M * t + m + 1)
                        wait(act, s_z2, M * t)
                        act.activation(h1_hi[:, m, 0:n], h1[:, m, 0:n], ACT.Copy).then_inc(s_h1_hi, 1)

            pipeline(act, step)

        @block.vector
        def _(dve):
            links = [0]

            def link(*together):
                links[0] += len(together)
                for ins in together:
                    ins.then_inc(s_idx, 1)
                dve.wait_ge(s_idx, links[0])

            to_tile = (
                lambda node: dve.tensor_scalar(g["tilet"][:, :], node[:, :], 0.5 - TILE / 2, 1.0 / TILE,
                                               ALU.add, ALU.mult),
                lambda: dve.tensor_scalar(g["tile"][:, :], g["tilet"][:, :], MAGIC, -MAGIC, ALU.add, ALU.add),
                lambda: dve.tensor_scalar(g["tile_half"][:, :], g["tile"][:, :], 0.5, -0.25, ALU.mult, ALU.add),
                lambda: dve.tensor_scalar(g["pair"][:, :], g["tile_half"][:, :], MAGIC, -MAGIC, ALU.add, ALU.add),
                lambda: dve.scalar_tensor_tensor(g["parity"][:, :], g["pair"][:, :], -2.0, g["tile"][:, :],
                                                 ALU.mult, ALU.add),
                lambda node: dve.scalar_tensor_tensor(g["offset"][:, :], g["tile"][:, :], -float(TILE), node[:, :],
                                                      ALU.mult, ALU.add),
                lambda: dve.scalar_tensor_tensor(g["offset2"][:, :], g["parity"][:, :], float(BANK), g["offset"][:, :],
                                                 ALU.mult, ALU.add))

            link(*[dve.memset(tile[:, :], 0) for tile in (g["base"], lowest, highest)])
            dve.wait_ge(s_pool_const, 13)
            link(dve.tensor_copy(window[:, :], window_i[:, :]),
                 dve.tensor_copy(g["centre"][:, :], centre_i[:, :]))
            for step_of_tile in to_tile:
                link(step_of_tile(g["centre"]) if step_of_tile in (to_tile[0], to_tile[5]) else step_of_tile())
            link(dve.tensor_copy(g["at_centre"][:, :], g["offset2"][:, :]))
            dve.wait_ge(s_dst, 64)
            row_sets = ((P, slice(0, FULL_ROWS)), (LAST_G, slice(FULL_ROWS, ROWS)))
            link(*[dve.tensor_copy(g["base"][0:r, c], dst_rows[0:r, c, 0]) for r, c in row_sets])
            for c in range(ROWS):
                r = P if c < FULL_ROWS else LAST_G
                dve.tensor_scalar(rel_rows[0:r, c, :], dst_rows[0:r, c, :], g["base"][0:r, c:c + 1], None,
                                  ALU.subtract).then_inc(s_relrow, 1)
            dve.wait_ge(s_relrow, ROWS)
            for r, c in row_sets:
                last = dve.tensor_reduce(lowest[0:r, c], rel_rows[0:r, c, :], AX.X, ALU.min)
            link(last)

            def onehot_of(i, parity, half):
                n, _ = groups_of(i, half)
                slot = 2 * parity + half
                cols = rel[:, :, :].rearrange("p g j -> p (g j)")[
                    :, bass.ds((i * GPT + half * HALF) * PER, n * PER)]
                return dve.tensor_tensor(onehot[:, slot, 0:n * PER, :],
                                         window[:, :].unsqueeze(1).broadcast_to([P, n * PER, WINDOW]),
                                         cols.unsqueeze(2).broadcast_to([P, n * PER, WINDOW]), ALU.is_equal)

            def make_onehot(i, parity, half):
                wait(dve, s_summed, NPARTS * (i - 2) + half + 2)
                onehot_of(i, parity, half).then_inc(s_onehot, 1)

            dve.wait_ge(s_rel, 1)
            make_onehot(0, 0, 0)
            for r, c in row_sets:
                last = dve.tensor_reduce(highest[0:r, c], rel_rows[0:r, c, :], AX.X, ALU.max)
            link(last)
            link(dve.tensor_tensor(g["drift"][:, :], g["base"][:, :], g["centre"][:, :], ALU.subtract), to_tile[0](g["base"]))
            link(dve.tensor_scalar(g["ok1"][:, :], g["drift"][:, :], -float(SLACK), None, ALU.is_ge), to_tile[1]())
            link(dve.scalar_tensor_tensor(g["ok2"][:, :], g["drift"][:, :], float(SLACK), g["ok1"][:, :],
                                          ALU.is_le, ALU.mult), to_tile[2]())
            link(dve.scalar_tensor_tensor(g["ok3"][:, :], g["base"][:, :], 0.0, g["ok2"][:, :],
                                          ALU.is_ge, ALU.mult), to_tile[3]())
            link(dve.scalar_tensor_tensor(g["ok4"][:, :], lowest[:, :], 0.0, g["ok3"][:, :], ALU.is_ge, ALU.mult),
                 to_tile[4]())
            link(dve.scalar_tensor_tensor(g["valid"][:, :], highest[:, :], float(WINDOW - 1), g["ok4"][:, :],
                                          ALU.is_le, ALU.mult), to_tile[5](g["base"]))
            link(dve.tensor_scalar(g["invalid"][:, :], g["valid"][:, :], -1.0, 1.0, ALU.mult, ALU.add),
                 to_tile[6]())
            link(dve.tensor_tensor(g["instead"][:, :], g["invalid"][:, :], g["at_centre"][:, :], ALU.mult),
                 dve.tensor_tensor(g["offset3"][:, :], g["offset2"][:, :], g["valid"][:, :], ALU.mult))
            dve.tensor_tensor(g["placed"][:, :], g["offset3"][:, :], g["instead"][:, :], ALU.add).then_inc(s_small, 1)
            make_onehot(0, 0, 1)
            dve.wait_ge(s_smallT, 1)
            dve.tensor_copy(offset_row[:, :], agg_ps[0:1, 0, :])
            dve.tensor_reduce(any_invalid[:, :], agg_ps[0:1, 1, :], AX.X, ALU.max).then_inc(s_off, 1)
            dve.wait_ge(s_b3, 2)
            dve.tensor_tensor(b3hilo[B3_LO:B3_LO + 1], b3raw[B3_LO:B3_LO + 1, :].unsqueeze(1).broadcast_to([1, PER, D]),
                              b3hi[B3_LO:B3_LO + 1, :].bitcast(F32).unsqueeze(1).broadcast_to([1, PER, D]),
                              ALU.subtract).then_inc(s_b3, 1)

            dve.wait_ge(s_rel, ROWS)

            def general_path():
                chain = [0]

                def step_of(ins):
                    chain[0] += 1
                    ins.then_inc(s_gen_chain, 1)
                    dve.wait_ge(s_gen_chain, chain[0])

                def turn(rounds, into, shift, sign):
                    for c in range(ROWS):
                        r = P if c < FULL_ROWS else LAST_G
                        dve.tensor_scalar(rel_rows[0:r, c, :], dst_rows[0:r, c, :], shift[0:r, c:c + 1], None,
                                          sign).then_inc(s_gen_rows, 1)
                    dve.wait_ge(s_gen_relT, ROWS * (rounds + 1))
                    for c in range(ROWS):
                        r = P if c < FULL_ROWS else LAST_G
                        ins = dve.tensor_copy(into[:, c * P:c * P + r, :],
                                              row_banks[c].rearrange("p (j r) -> p r j", j=PER)[:, 0:r, :])
                    step_of(ins)

                dve.wait_ge(s_relT, ROWS)
                step_of(dve.tensor_scalar(g["ok1"][:, :], g["valid"][:, :], FAR, None, ALU.mult))
                step_of(dve.scalar_tensor_tensor(g["shift"][:, :], g["invalid"][:, :], FAR, g["base"][:, :],
                                                 ALU.mult, ALU.add))
                step_of(dve.tensor_copy(tile_cols, tile_i))
                dve.wait_ge(s_carry0, 1)
                turn(0, gen_rel, g["ok1"], ALU.add)
                dve.wait_ge(s_onehot, 2)
                turn(1, rel, g["shift"], ALU.subtract)
                dve.wait_ge(s_summed, 1)
                for half in range(2):
                    step_of(onehot_of(0, 0, half))
                before = chain[0]

                def group(gr):
                    dve.tensor_copy(gen_cols[:, :], gen_rel[:, bass.ds(gr, 1), :].rearrange(
                        "p g j -> p (g j)")).then_inc(s_gen_chain, 1)
                    with dve.Fori(0, NT) as n:
                        dve.wait_ge(s_gen_chain, gr * (2 * NT + 1) + 2 * n + 1 + before)
                        for j in range(PER):
                            ins = dve.tensor_scalar(gen_onehot[:, j, :], tile_cols[:, :], gen_cols[:, j:j + 1], None,
                                                    ALU.is_equal)
                        ins.then_inc(s_gen_onehot, 1)
                        dve.wait_ge(s_gen_sum, gr * NT + n + 1)
                        into = agg_carry[0:ED, bass.ds(n * TILE, TILE)]
                        dve.tensor_tensor(into, z3[0:ED, :, :].rearrange("p q d -> p (q d)")[:, 0:TILE], into,
                                          ALU.add).then_inc(s_gen_chain, 1)
                        dve.wait_ge(s_gen_onehot, gr * NT + n + 1)
                        dve.tensor_scalar(gen_cols[:, :], gen_cols[:, :], -float(TILE), None,
                                          ALU.add).then_inc(s_gen_chain, 1)
                    dve.wait_ge(s_gen_chain, gr * (2 * NT + 1) + 2 * NT + 1 + before)

                with dve.Fori(0, NG) as gr:
                    group(gr)
                dve.wait_ge(s_resummed, 1)

            where_invalid(dve, mybir.EngineType.DVE, general_path)

            def stage_sums(i, parity, s):
                a, b = part_of(i, s)
                k = (parity + s) % 2
                dve.wait_ge(s_summed, NPARTS * i + s + 1)
                wait(dve, s_placed, NPARTS * i + s - 1)
                dve.tensor_reduce(staged[0:WINDOW, k, 0:b - a, :],
                                  stage[0:WINDOW, k, 0:2 * ED * (b - a)].rearrange("w (g h d) -> w g d h", h=2, d=ED),
                                  AX.X, ALU.add).then_inc(s_staged, 1)

            def step(i, parity):
                np_ = nodes_p(i)
                if has(i, 0, NT):
                    stage_sums(i, parity, 0)
                    dve.wait_ge(s_x[parity], 16 * slot_turn(i, parity) + (16 if np_ != TP else 0))
                    wait(dve, s_rstd, i - 1)
                    for q in range(PER):
                        st = dve.bn_stats(stats[0:np_, q, :], x_t[0:np_, parity, q, :])
                    st.then_inc(s_stats, 1)
                    dve.wait_ge(s_stats, i + 1)
                if has(i, 1, NT):
                    t, tp_ = i - 1, nodes_p(i - 1)
                    dve.wait_ge(s_hT, t + 1)
                    wait(dve, s_z1, M * t)
                    dve.scalar_tensor_tensor(hT_lo[:, 0:PER * tp_].rearrange("d (p q) -> d q p", q=PER),
                                             tp[:, 0:PER * tp_].rearrange("d (q p) -> d q p", q=PER), 0.0,
                                             hT_hi[:, 0:PER * tp_].bitcast(F32).rearrange("d (p q) -> d q p", q=PER),
                                             ALU.max, ALU.subtract).then_inc(s_hT_lo, 1)
                if has(i, 0, NT):
                    for q in range(PER):
                        mv = dve.bn_aggr(meanvar[0:np_, parity, q, :], stats[0:np_, q, :])
                    mv.then_inc(s_mv, 1)
                if has(i, -1, NT):
                    make_onehot(i + 1, 1 - parity, 0)
                if has(i, 0, NT):
                    stage_sums(i, parity, 1)
                if has(i, 1, NT):
                    t, n = i - 1, PER * nodes_p(i - 1)
                    if isinstance(t, int) and t == NT - 1:
                        dve.wait_ge(s_placed, NPARTS * NT)
                    else:
                        dve.wait_ge(s_closed, t + 1)
                    dve.wait_ge(s_carry0, 1)
                    wait(dve, s_carried, t)
                    wait(dve, s_agg_lo, t)
                    dve.tensor_tensor(agg[:, 0:n], agg_ps[0:ED, 1 - parity, 0:n],
                                      agg_carry[:, bass.ds(t * TILE, n)], ALU.add).then_inc(s_agg, 1)
                    if has(i, 1, NT - 1):
                        over = agg_carry[:, bass.ds((t + 1) * TILE, OVER)]
                        dve.tensor_tensor(over, agg_ps[0:ED, 1 - parity, TILE:BANK], over,
                                          ALU.add).then_inc(s_carried, 1)
                    dve.wait_ge(s_agg_hi, t + 1)
                    dve.tensor_tensor(agg_hilo[ROW2:ROW2 + ED, 0:n], agg[:, 0:n], agg_hilo[0:ED, 0:n].bitcast(F32),
                                      ALU.subtract).then_inc(s_agg_lo, 1)
                if has(i, 2, NT):
                    t, tp_ = i - 2, nodes_p(i - 2)
                    dve.wait_ge(s_z3, t + 1)
                    dve.wait_ge(s_resid, t + 1)
                    wait(dve, s_stored[parity], 16 * (slot_turn(t, parity) - 1))
                    dve.tensor_tensor(out_t[0:tp_, parity], z3[0:tp_, :, :], resid[0:tp_, parity],
                                      ALU.add).then_inc(s_out, 1)
                if has(i, 0, NT):
                    stage_sums(i, parity, 2)
                if has(i, -1, NT):
                    make_onehot(i + 1, 1 - parity, 1)
                if has(i, 0, NT):
                    dve.wait_ge(s_rstd, i + 1)
                    wait(dve, s_tp, i - 1)
                    for q in range(PER):
                        ln = dve.tensor_scalar(xn[0:np_, parity, q, :], x_t[0:np_, parity, q, :],
                                               meanvar[0:np_, parity, q, 0:1], rstd[0:np_, parity, q:q + 1],
                                               ALU.subtract, ALU.mult)
                    ln.then_inc(s_xn, 1)
                    dve.wait_ge(s_xn, i + 1)
                    wait(dve, s_out, i - 1)
                    dve.scalar_tensor_tensor(resid[0:np_, parity].rearrange("p q d -> p (q d)"),
                                             xn[0:np_, parity].rearrange("p q d -> p (q d)"), 0.0,
                                             x_t[0:np_, parity].rearrange("p q d -> p (q d)"),
                                             ALU.max, ALU.add).then_inc(s_resid, 1)

            pipeline(dve, step)

        @block.tensor
        def _(pe):
            pe.wait_ge(s_pool_const, 13)
            n_groups = [P] * FULL_ROWS + [LAST_G]
            for c, r in enumerate(n_groups):
                pe.wait_ge(s_relrow, c + 1)
                for j in range(PER):
                    tr = pe.transpose(row_banks[c][:, j * P:j * P + r],
                                      rel_rows[0:r, c, :].rearrange("r (p j) -> r j p", j=PER)[:, j, :],
                                      ident[0:r, 0:r])
                tr.then_inc(s_relT, 1)

            def one_hot_sums(i, parity, s):
                a, b = part_of(i, s)
                bank = (parity + s) % 2
                for k in range(a, b):
                    half = k // HALF
                    full = groups_of(i, half)[1]
                    rows = P if k - half * HALF < full else TAIL_P
                    slot = 2 * parity + half
                    if k == a or k == HALF:
                        pe.wait_ge(s_lo, 2 * i + half + 1)
                        pe.wait_ge(s_onehot, 2 * i + half + 1)
                    for j in range(PER):
                        c = 2 * ED * (k - a)
                        mm = pe.matmul(stage[0:WINDOW, bank, c:c + 2 * ED],
                                       onehot[0:rows, slot, (k - half * HALF) * PER + j, :],
                                       hilo[0:rows, slot, k - half * HALF, j].rearrange("p h d -> p (h d)"),
                                       start=(k == a and j == 0), stop=True, skip_group_check=True)
                return mm

            def sum_groups(i, parity, s):
                wait(pe, s_staged, NPARTS * i + s - 1)
                one_hot_sums(i, parity, s).then_inc(s_summed, 1)

            sum_groups(0, 0, 0)
            pe.wait_ge(s_small, 1)
            for c in range(ROWS):
                pe.matmul(agg_ps[0:1, 0, c * P:(c + 1) * P], g["placed"][:, c:c + 1], ident[:, :],
                          start=True, stop=True)
            for c, r in enumerate(n_groups):
                small = pe.matmul(agg_ps[0:1, 1, c * P:(c + 1) * P], g["invalid"][0:r, c:c + 1], ident[0:r, :],
                                  start=True, stop=True)
            small.then_inc(s_smallT, 1)

            def general_path():
                for rounds in range(2):
                    for c, r in enumerate(n_groups):
                        pe.wait_ge(s_gen_rows, ROWS * rounds + c + 1)
                        for j in range(PER):
                            tr = pe.transpose(row_banks[c][:, j * P:j * P + r],
                                              rel_rows[0:r, c, :].rearrange("r (p j) -> r j p", j=PER)[:, j, :],
                                              ident[0:r, 0:r])
                        tr.then_inc(s_gen_relT, 1)
                pe.wait_ge(s_gen_chain, 7)
                one_hot_sums(0, 0, 0).then_inc(s_resummed, 1)

                def group(gr, rows):
                    with pe.Fori(0, NT) as n:
                        pe.wait_ge(s_gen_raw, (gr + 1) * 16)
                        pe.wait_ge(s_gen_onehot, gr * NT + n + 1)
                        for j in range(PER):
                            mm = pe.matmul(z3[0:ED, :, :].rearrange("p q d -> p (q d)")[:, 0:TILE],
                                           gen_raw[0:rows, j, :], gen_onehot[0:rows, j, :].bitcast(F32),
                                           start=(j == 0), stop=(j == PER - 1))
                        mm.then_inc(s_gen_sum, 1)

                with pe.Fori(0, NG - 1) as gr:
                    group(gr, P)
                group(NG - 1, TAIL_P)

            where_invalid(pe, mybir.EngineType.PE, general_path)
            banks = agg_ps[:, :, :].rearrange("p k n -> p (k n)")
            pe.wait_ge(s_clear, 2)

            def place_groups(i, parity, s, offsets):
                a, b = part_of(i, s)
                pe.wait_ge(s_staged, NPARTS * i + s + 1)
                for k in range(a, b):
                    if k == GPT - EARLY and has(i, -1, NT):
                        pe.wait_ge(s_clear, i + 2)
                    mm = pe.matmul(banks[0:ED, bass.ds(offsets[k - a], WINDOW)],
                                   staged[:, (parity + s) % 2, k - a, :], ident[0:PLACE_K, 0:WINDOW],
                                   start=False, stop=True, skip_group_check=True)
                    if k == EARLY - 1 and has(i, 1, NT):
                        mm.then_inc(s_closed, 1)
                mm.then_inc(s_placed, 1)

            def step(i, parity):
                before = part_of(i - 1, 2)[1] - PARTS[2][0] if has(i, 1, NT) else 0
                first_group = i * GPT - before if isinstance(i, int) and i < NT else i * GPT - (GPT - PARTS[2][0])
                count = before + (PARTS[1][1] if has(i, 0, NT) else 0)
                if count:
                    _, offs = nc.values_load_multi_w_load_instructions(
                        offset_row[0:1, bass.ds(first_group, count)], engines=[mybir.EngineType.PE],
                        min_val=0, max_val=2 * BANK - WINDOW,
                        skip_runtime_bounds_check_because="valid groups lie within SLACK of their tile")
                if has(i, 0, NT) and not (isinstance(i, int) and i == 0):
                    sum_groups(i, parity, 0)
                if has(i, 1, NT):
                    place_groups(i - 1, 1 - parity, 2, offs[:before])
                    t, np_ = i - 1, nodes_p(i - 1)
                    pe.wait_ge(s_xn, t + 1)
                    wait(pe, s_hT_lo, t)
                    for q in range(PER):
                        tr = pe.transpose(tp[:, q * np_:(q + 1) * np_], xn[0:np_, 1 - parity, q, :],
                                          ident[0:np_, 0:np_])
                    tr.then_inc(s_tp, 1)
                if has(i, 2, NT):
                    t, n = i - 2, PER * nodes_p(i - 2)
                    for k in range(M):
                        pe.wait_ge(s_h1_hi, M * t + k + 1)
                        for m in range(M):
                            if k == 0:
                                pe.wait_ge(s_h1, M * t + m + 1)
                            pe.matmul(z[:, m, 0:n], w2_hi[:, k, m * P:(m + 1) * P], h1_hi[:, k, 0:n],
                                      start=(k == 0), stop=False)
                            pe.matmul(z[:, m, 0:n], w2_lo[:, k, m * P:(m + 1) * P], h1_hi[:, k, 0:n],
                                      start=False, stop=False)
                    for m in range(M):
                        for k in range(M):
                            if m == 0:
                                pe.wait_ge(s_h1_lo, M * t + k + 1)
                            mm = pe.matmul(z[:, m, 0:n], w2_hi[:, k, m * P:(m + 1) * P], h1_lo[:, k, 0:n],
                                           start=False, stop=(k == M - 1))
                        mm.then_inc(s_z2, 1)
                if has(i, 0, NT):
                    sum_groups(i, parity, 1)
                    place_groups(i, parity, 0, offs[before:])
                if has(i, 2, NT):
                    t, np_ = i - 2, nodes_p(i - 2)
                    wait(pe, s_out, t)
                    if isinstance(t, int) and t == 0:
                        pe.wait_ge(s_b3, 4)
                    pe.matmul(z3[0:np_, :, :].rearrange("p q d -> p (q d)"), ones_r[:, 0:np_],
                              b3hilo[:, :, :].rearrange("p q d -> p (q d)"),
                              start=True, stop=False, skip_group_check=True)
                    pe.wait_ge(s_h2, M * t + M)
                    for q in range(PER):
                        for k in range(M):
                            mm = pe.matmul(z3[0:np_, q, :],
                                           h2[:, k, 0:PER * np_].rearrange("c (p q) -> c q p", q=PER)[:, q, :],
                                           w3[:, k, :], start=False, stop=(q == PER - 1 and k == M - 1),
                                           skip_group_check=True)
                    mm.then_inc(s_z3, 1)
                if has(i, 0, NT):
                    sum_groups(i, parity, 2)
                    place_groups(i, parity, 1, offs[before + PARTS[0][1]:])
                if has(i, 1, NT):
                    t, n = i - 1, PER * nodes_p(i - 1)
                    pe.wait_ge(s_hT_lo, t + 1)
                    if isinstance(t, int) and t == 0:
                        pe.wait_ge(s_w_lo, 3)
                        pe.wait_ge(s_w_hi, 4)
                        pe.wait_ge(s_const, CONSTS)
                    for m in range(M):
                        wait(pe, s_h2, M * (t - 1) + m + 1)
                        for w, act_ in ((w1x_hi, hT_hi), (w1x_lo, hT_hi), (w1x_hi, hT_lo)):
                            pe.matmul(z[:, m, 0:n], w[:, m * P:(m + 1) * P], act_[:, 0:n],
                                      start=(w is w1x_hi and act_ is hT_hi), stop=False)
                    pe.wait_ge(s_agg_lo, t + 1)
                    for m in range(M):
                        pe.matmul(z[:, m, 0:n], w1e_hi[:, m * P:(m + 1) * P], agg_hilo[:, 0:n],
                                  start=False, stop=False)
                        pe.matmul(z[:, m, 0:n], w1e_lo[:, m * P:(m + 1) * P], agg_hilo[0:ED, 0:n],
                                  start=False, stop=True).then_inc(s_z1, 1)

            pipeline(pe, step)


_INS = ["x", "dst", "edge_attr_48", "L0_gnn_W1", "L0_gnn_b1", "L0_gnn_W2", "L0_gnn_b2", "L0_gnn_W3", "L0_gnn_b3"]


def kernel(**inputs):
    import numpy as _np
    import concourse.bacc as _bacc
    from concourse import mybir as _mybir
    from concourse.bass_utils import run_bass_kernel_spmd as _run

    nc = _bacc.Bacc("TRN2", target_bir_lowering=False, num_devices=1)
    arrays, args = {}, []
    for name in _INS:
        a = _np.ascontiguousarray(inputs[name])
        arrays[f"in_{name}_dram"] = a
        args.append(nc.dram_tensor(f"in_{name}_dram", a.shape, _mybir.dt.from_np(a.dtype), kind="ExternalInput").ap())
    out = nc.dram_tensor("out_0_dram", inputs["x"].shape, _mybir.dt.float32, kind="ExternalOutput").ap()
    gnn_kernel(nc, *args, out)
    r = _run(nc, [arrays], core_ids=[0])
    return r.results[0]["out_0_dram"]
```

```python
from contextlib import ExitStack

import concourse.bass as bass
from concourse import mybir

ALU = mybir.AluOpType
ACT = mybir.ActivationFunctionType
AX = mybir.AxisListType
F32 = mybir.dt.float32
F32R = mybir.dt.float32r
I32 = mybir.dt.int32


def gnn_kernel(nc, x, dst, edge_attr, W1, b1, W2, b2, W3, b3, out):
    N, D = x.shape
    E, ED = edge_attr.shape
    HID = W1.shape[1]
    P = 128
    M = HID // P
    EPS = 1e-5

    PER = 4
    GROUP = P * PER
    NG = -(-E // GROUP)
    TAIL_P = (E - (NG - 1) * GROUP) // PER
    NPG = GROUP * N // E
    GPT = 14
    HALF = GPT // 2
    PARTS = ((0, 5), (5, 10), (10, GPT))
    NPARTS = len(PARTS)
    PART = 5
    TILE = NPG * GPT
    TP = TILE // PER
    NT = -(-N // TILE)
    LAST_P = (N - (NT - 1) * TILE) // PER
    BANK = 512
    OVER = BANK - TILE
    WINDOW = 42
    REACH = (WINDOW - 1) / 2
    EARLY = 3
    SLACK = EARLY * NPG
    ROWS = 4
    FULL_ROWS = NG // P
    LAST_G = NG - FULL_ROWS * P
    FAR = float(1 << 20)
    PLACE_K = 96
    ROW2 = 64
    MAGIC = 1.5 * 2.0 ** 23
    assert N * GROUP == NPG * E and E % PER == 0 and N % PER == 0
    assert WINDOW <= OVER and 2 * ED * PART <= BANK and FULL_ROWS == ROWS - 1

    LOOP_FIRST, LOOP_END = 4, 24
    STEPS = NT + 2

    def groups_of(i, half):
        g0 = i * GPT + half * HALF if isinstance(i, int) else 0
        n = min(HALF, NG - g0)
        return n, min(n, NG - 1 - g0)

    def part_of(i, s):
        a, b = PARTS[s]
        return a, min(b, NG - i * GPT) if isinstance(i, int) else b

    def nodes_p(t):
        return LAST_P if isinstance(t, int) and t == NT - 1 else TP

    with ExitStack() as ctx:
        def sb(name, shape, dt=F32):
            return ctx.enter_context(nc.sbuf_tensor(name, shape, dt))

        def ps(name, shape, dt=F32):
            return ctx.enter_context(nc.psum_tensor(name, shape, dt))

        def sem(name):
            return ctx.enter_context(nc.semaphore(name))

        w1x_hi = sb("w1x_hi", [D, HID], F32R)
        w1x_lo = sb("w1x_lo", [D, HID], F32R)
        w1e_hi = sb("w1e_hi", [ROW2 + ED, HID], F32R)
        w1e_lo = sb("w1e_lo", [ED, HID], F32R)
        w2_hi = sb("w2_hi", [P, M, HID], F32R)
        w2_lo = sb("w2_lo", [P, M, HID], F32R)
        w3 = sb("w3", [P, M, D])
        b1c = sb("b1c", [P, M])
        b2c = sb("b2c", [P, M])
        b3r = sb("b3r", [P, D])
        zeros = sb("zeros", [P, 1])
        silu_try = sb("silu_try", [P, 1])
        ident = sb("ident", [P, P])
        one = sb("one", [P, 1])
        window_i = sb("window_i", [P, WINDOW], I32)
        window = sb("window", [P, WINDOW])
        minus_half = sb("minus_half", [P, PER])
        eps = sb("eps", [P, PER])

        dst_rows = sb("dst_rows", [P, ROWS, GROUP], I32)
        rel_rows = sb("rel_rows", [P, ROWS, GROUP])
        farthest = sb("farthest", [P, ROWS])
        centre_i = sb("centre_i", [P, ROWS], I32)
        g = {n: sb("g_" + n, [P, ROWS]) for n in (
            "base", "middle", "centre", "drift", "ok1", "ok2", "ok3", "valid", "invalid",
            "tile", "tilet", "tile_half", "pair", "parity", "offset", "offset2", "offset3",
            "at_centre", "instead", "placed", "shift")}
        rel = sb("rel", [P, NG, PER])
        offset_row = sb("offset_row", [1, ROWS * P], I32)
        any_invalid = sb("any_invalid", [1, 1], I32)

        raw = sb("raw", [P, 4, HALF, PER, ED])
        hilo = sb("hilo", [P, 4, HALF, PER, 2, ED], F32R)
        onehot = sb("onehot", [P, 4, HALF * PER, WINDOW], F32R)
        staged = sb("staged", [PLACE_K, 2, PART, ED])
        agg_carry = sb("agg_carry", [ED, NT * TILE + OVER])

        POOL_ZEROS = 11 * TILE

        gen_onehot = onehot[:, 2:4].rearrange("p s e w -> p (s e w)")[:, 0:PER * TILE].rearrange(
            "p (j n) -> p j n", j=PER)

        x_t = sb("x_t", [P, 2, PER, D])
        stats = sb("stats", [P, PER, 6])
        meanvar = sb("meanvar", [P, 2, PER, 2])
        vareps = sb("vareps", [P, PER])
        rstd = sb("rstd", [P, 2, PER])
        nmr = sb("nmr", [P, 2, PER])
        xn = sb("xn", [P, 2, PER, D])
        resid = sb("resid", [P, 2, PER, D])
        hT_hi = sb("hT_hi", [D, TILE], F32R)
        hT_lo = sb("hT_lo", [D, TILE], F32R)
        agg = sb("agg", [ED, TILE])
        agg_hilo = sb("agg_hilo", [ROW2 + ED, TILE], F32R)
        h = sb("h", [P, 2 * M, TILE])
        h1, h2 = h[:, 0:M], h[:, M:2 * M]
        h1_hi = sb("h1_hi", [P, M, TILE], F32R)
        h1_lo = sb("h1_lo", [P, M, TILE], F32R)
        ones = resid[:, 1, 0, :]
        out_t = sb("out_t", [P, 2, PER, D])
        load_w = out_t[:, :, :, :].rearrange("p k q d -> p (k q d)")
        w2_in = load_w[:, 0:M * HID].rearrange("p (m n) -> p m n", m=M)
        w1x_in = load_w[:, M * HID:(M + 1) * HID]
        w1e_in = load_w[0:ROW2 + ED, (M + 1) * HID:(M + 2) * HID]

        gen_rel = h[:, :, :].rearrange("p m n -> p (m n)")[:, 0:NG * PER].rearrange(
            "p (g j) -> p g j", j=PER)
        tables = xn[:, :, :, :].rearrange("p k q d -> p (k q d)")
        tile_cols = tables[:, 0:TILE]
        tile_i = tables[:, TILE:2 * TILE].bitcast(I32)
        gen_raw = resid[:, 0].rearrange("p q d -> p (q d)")[:, 0:PER * ED].rearrange("p (j d) -> p j d", j=PER)
        gen_cols = sb("gen_cols", [P, PER])

        agg_ps = ps("agg_ps", [P, 2, BANK])
        tp = ps("tp", [P, BANK])
        stage = ps("stage", [P, 2, BANK])
        z = ps("z", [P, M, BANK])
        z3 = ps("z3", [P, PER, D])
        row_banks = (z[:, 0, :], z[:, 1, :], z3[:, :, :].rearrange("p q d -> p (q d)"), tp[:, :])

        s_const = sem("const_loaded")
        s_dst = sem("dst_loaded")
        s_pool_const = sem("pool_const")
        s_idx = sem("index_step")
        s_small = sem("small_ready")
        s_smallT = sem("small_transposed")
        s_off = sem("offsets_ready")
        s_relrow = sem("rel_rows_ready")
        s_relT = sem("rel_transposed")
        s_rel = sem("rel_ready")
        s_gen_rows = sem("general_rows")
        s_gen_relT = sem("general_transposed")
        s_gen_raw = sem("general_edges_loaded")
        s_gen_onehot = sem("general_onehot")
        s_resummed = sem("first_part_resummed")
        s_gen_sum = sem("general_summed")
        s_gen_chain = sem("general_chain")
        s_carry0 = sem("carry_zeroed")
        s_carry0_dma = sem("carry_zeroed_by_dma")
        s_edges = [sem(f"edges_loaded{k}") for k in range(4)]
        s_hi = sem("hi_ready")
        s_lo = sem("lo_ready")
        s_onehot = sem("onehot_ready")
        s_summed = sem("part_summed")
        s_staged = sem("part_staged")
        s_placed = sem("part_placed")
        s_closed = sem("bank_closed")
        s_clear = sem("bank_clear")
        s_agg = sem("agg_ready")
        s_agg_hi = sem("agg_hi_ready")
        s_agg_lo = sem("agg_lo_ready")
        s_w_hi = sem("weights_hi_ready")
        s_w_lo = sem("weights_lo_ready")
        s_carried = sem("overhang_carried")
        s_x = [sem(f"x_loaded{k}") for k in range(2)]
        s_stats = sem("stats_ready")
        s_mv = sem("meanvar_ready")
        s_eps = sem("vareps_ready")
        s_rstd = sem("rstd_ready")
        s_nmr = sem("minus_mean_rstd_ready")
        s_plain = sem("resid_without_b3")
        s_xn = sem("xn_ready")
        s_resid = sem("resid_ready")
        s_tp = sem("transposed")
        s_hT = sem("hT_hi_ready")
        s_hT_lo = sem("hT_lo_ready")
        s_z1 = sem("z1_ready")
        s_h1 = sem("h1_ready")
        s_h1_hi = sem("h1_hi_ready")
        s_h1_lo = sem("h1_lo_ready")
        s_z2 = sem("z2_ready")
        s_h2 = sem("h2_ready")
        s_z3 = sem("z3_ready")
        s_out = sem("out_ready")
        s_stored = [sem(f"out_stored{k}") for k in range(2)]

        block = ctx.enter_context(nc.Block())

        def wait(eng, s, count):
            if isinstance(count, int) and count <= 0:
                return
            eng.wait_ge(s, count)

        def pipeline(eng, step):
            for i in range(LOOP_FIRST):
                step(i, i % 2)
            with eng.Fori(LOOP_FIRST, LOOP_END, 2) as i:
                for u in range(2):
                    step(i + u, u)
            for i in range(LOOP_END, STEPS):
                step(i, i % 2)

        def where_invalid(eng, engine_type, body):
            eng.wait_ge(s_off, 1)
            _, (flag,) = nc.values_load_multi_w_load_instructions(
                any_invalid[0:1, 0:1], engines=[engine_type], min_val=0, max_val=NG,
                skip_runtime_bounds_check_because="it counts groups")
            with eng.If(flag):
                body()

        def has(i, lag, count):
            return not isinstance(i, int) or 0 <= i - lag < count

        def slot_turn(i, parity):
            return (i - parity) // 2 + 1

        def h1_lo_part(eng, t):
            n = PER * nodes_p(t)
            for m in range(M):
                eng.wait_ge(s_h1_hi, M * t + m + 1)
                wait(eng, s_z2, M * t)
                if isinstance(t, int) and t == NT - 1:
                    eng.wait_ge(s_h1_lo, M * t)
                eng.tensor_tensor(h1_lo[:, m, 0:n], h1[:, m, 0:n], h1_hi[:, m, 0:n].bitcast(F32),
                                  ALU.subtract).then_inc(s_h1_lo, 1)

        def layer1_banks(t):
            return stage if isinstance(t, int) and t == NT - 1 else z

        @block.sync
        def _(sp):
            rows = dst[0:FULL_ROWS * P * GROUP].rearrange("(c r e) -> r c e", r=P, e=GROUP)
            sp.dma_start(dst_rows[:, 0:FULL_ROWS, :], rows).then_inc(s_dst, 16)
            d0 = FULL_ROWS * P * GROUP
            sp.dma_start(dst_rows[0:LAST_G - 1, FULL_ROWS, :],
                         dst[d0:d0 + (LAST_G - 1) * GROUP].rearrange("(r e) -> r e", e=GROUP)).then_inc(s_dst, 16)
            n = TAIL_P * PER
            sp.dma_start(dst_rows[LAST_G - 1:LAST_G, FULL_ROWS, 0:n],
                         dst[E - n:E].rearrange("(r e) -> r e", r=1)).then_inc(s_dst, 16)
            sp.dma_start(dst_rows[LAST_G - 1:LAST_G, FULL_ROWS, n:GROUP],
                         dst[E - (GROUP - n):E].rearrange("(r e) -> r e", r=1)).then_inc(s_dst, 16)

            def load_edges(i, parity, half):
                n, full = groups_of(i, half)
                slot = 2 * parity + half
                wait(sp, s_lo, 2 * (i - 2) + half + 1)
                e0 = (i * GPT + half * HALF) * GROUP
                sp.dma_start(raw[:, slot, 0:full].rearrange("p g j d -> p g (j d)"),
                             edge_attr[bass.ds(e0, full * GROUP), :].rearrange(
                                 "(g p j) d -> p g (j d)", p=P, j=PER)).then_inc(s_edges[slot], 16)
                if full < n:
                    sp.dma_start(raw[0:TAIL_P, slot, full].rearrange("p j d -> p (j d)"),
                                 edge_attr[E - TAIL_P * PER:E, :].rearrange(
                                     "(p j) d -> p (j d)", j=PER)).then_inc(s_edges[slot], 16)

            def load_x(t, parity):
                wait(sp, s_resid, t - 1)
                np_ = nodes_p(t)
                for a, b in ([(0, TP)] if np_ == TP else [(0, 96), (96, np_)]):
                    sp.dma_start(x_t[a:b, parity].rearrange("p q d -> p (q d)"),
                                 x[bass.ds(t * TILE + a * PER, (b - a) * PER), :].rearrange(
                                     "(p q) d -> p (q d)", q=PER)).then_inc(s_x[parity], 16)

            for half in range(2):
                load_edges(0, 0, half)
            load_x(0, 0)
            sp.dma_start(w2_in, W2.rearrange("(m p) n -> p m n", p=P)).then_inc(s_const, 16)
            sp.dma_start(w1x_in, W1[0:D, :]).then_inc(s_const, 16)
            for a in (0, ROW2):
                sp.dma_start(w1e_in[a:a + ED, :], W1[D:D + ED, :]).then_inc(s_const, 16)
            sp.dma_start(w3[:, :, :], W3.rearrange("(m p) n -> p m n", p=P)).then_inc(s_const, 16)
            sp.dma_start(b1c[:, :], b1.rearrange("(m p) -> p m", p=P), allow_slow_non_contiguous=True).then_inc(s_const, 16)
            sp.dma_start(b2c[:, :], b2.rearrange("(m p) -> p m", p=P), allow_slow_non_contiguous=True).then_inc(s_const, 16)
            sp.dma_start(b3r[:, :], b3.rearrange("(r n) -> r n", r=1).broadcast_to([P, D])).then_inc(s_const, 16)
            for half in range(2):
                load_edges(1, 1, half)
            load_x(1, 1)
            sp.wait_ge(s_pool_const, 11)
            zero_tile = agg_hilo[0:ED, :].bitcast(F32)
            tiles = NT - POOL_ZEROS // TILE
            sp.dma_start(agg_carry[:, POOL_ZEROS:NT * TILE].rearrange("d (t n) -> d t n", n=TILE),
                         zero_tile.unsqueeze(1).broadcast_to([ED, tiles, TILE])).then_inc(s_carry0_dma, 16)
            sp.dma_start(agg_carry[:, NT * TILE:], zero_tile[:, 0:OVER]).then_inc(s_carry0_dma, 16)

            def general_loads():
                def load(gr, rows):
                    sp.dma_start(gen_raw[0:rows].rearrange("p j d -> p (j d)"),
                                 edge_attr[bass.ds(gr * GROUP, rows * PER), :].rearrange(
                                     "(p j) d -> p (j d)", j=PER)).then_inc(s_gen_raw, 16)

                load(0, P)
                with sp.Fori(1, NG - 1) as gr:
                    sp.wait_ge(s_gen_sum, gr * NT)
                    load(gr, P)
                sp.wait_ge(s_gen_sum, (NG - 1) * NT)
                load(NG - 1, TAIL_P)

            where_invalid(sp, mybir.EngineType.SP, general_loads)

            def step(i, parity):
                if has(i, -2, NT):
                    for half in range(2):
                        load_edges(i + 2, parity, half)
                if has(i, -1, NT) and not (isinstance(i, int) and i == 0):
                    load_x(i + 1, 1 - parity)
                if has(i, 2, NT):
                    t = i - 2
                    sp.wait_ge(s_out, t + 1)
                    np_ = nodes_p(t)
                    for a, b in ([(0, TP)] if np_ == TP else [(0, 96), (96, np_)]):
                        sp.dma_start(out[bass.ds(t * TILE + a * PER, (b - a) * PER), :].rearrange(
                            "(p q) d -> p (q d)", q=PER),
                            out_t[a:b, parity].rearrange("p q d -> p (q d)")).then_inc(s_stored[parity], 16)

            pipeline(sp, step)
            sp.wait_ge(s_stored[0], 16 * (NT // 2))
            sp.wait_ge(s_stored[1], 16 * (NT // 2 + 1))

        CONSTS = 16 * 8

        @block.gpsimd
        def _(pool):
            pool.memset(ones, 1.0).then_inc(s_pool_const, 1)
            pool.iota(window_i[:, :], pattern=[[1, WINDOW]], base=0, channel_multiplier=0).then_inc(s_pool_const, 1)
            pool.iota(centre_i[:, :], pattern=[[NPG * P, ROWS]], base=0,
                      channel_multiplier=NPG).then_inc(s_pool_const, 1)
            pool.iota(tile_i[:, :], pattern=[[1, TILE]], base=0, channel_multiplier=0).then_inc(s_pool_const, 1)
            pool.memset(minus_half[:, :], -0.5).then_inc(s_pool_const, 1)
            pool.memset(eps[:, :], EPS).then_inc(s_pool_const, 1)
            pool.memset(one[:, :], 1.0).then_inc(s_pool_const, 1)
            pool.memset(agg_hilo[:, :].bitcast(F32), 0.0).then_inc(s_pool_const, 1)
            pool.memset(w1e_hi[:, :].bitcast(F32), 0.0).then_inc(s_pool_const, 1)
            pool.memset(zeros[:, :], 0.0).then_inc(s_pool_const, 1)
            pool.memset(staged[:, :, :, :], 0.0).then_inc(s_pool_const, 1)
            pool.wait_ge(s_pool_const, 11)
            pool.affine_select(out=ident[:, :], in_=ones, compare_op=ALU.is_equal, fill=0.0, base=0,
                               pattern=[[-1, P]], channel_multiplier=1).then_inc(s_pool_const, 1)
            pool.memset(agg_carry[:, 0:POOL_ZEROS], 0.0).then_inc(s_carry0, 1)

            def lo_part(i, parity, half):
                n, full = groups_of(i, half)
                slot = 2 * parity + half
                pool.wait_ge(s_hi, 2 * i + half + 1)
                for p, a, b in [(P, 0, full)] + ([(TAIL_P, full, n)] if full < n else []):
                    lo = pool.tensor_tensor(
                        hilo[0:p, slot, a:b, :, 1, :].rearrange("p g j d -> p (g j) d"),
                        raw[0:p, slot, a:b].rearrange("p g j d -> p (g j) d"),
                        hilo[0:p, slot, a:b, :, 0, :].rearrange("p g j d -> p (g j) d").bitcast(F32),
                        ALU.subtract)
                lo.then_inc(s_lo, 1)

            def make_rstd(i, parity):
                np_ = nodes_p(i)
                pool.wait_ge(s_mv, i + 1)
                wait(pool, s_xn, i - 1)
                pool.tensor_tensor(vareps[0:np_, :], meanvar[0:np_, parity, :, 1], eps[0:np_, :],
                                   ALU.add).then_inc(s_eps, 1)
                pool.wait_ge(s_eps, i + 1)
                pool.tensor_tensor(rstd[0:np_, parity], vareps[0:np_, :], minus_half[0:np_, :],
                                   ALU.pow).then_inc(s_rstd, 1)

            for half in range(2):
                lo_part(0, 0, half)

            def step(i, parity):
                rstd_turn = 1 if isinstance(i, int) and i < 2 else 0
                for half in range(2):
                    if has(i, 0, NT) and half == rstd_turn:
                        make_rstd(i, parity)
                    if has(i, -1, NT):
                        lo_part(i + 1, 1 - parity, half)
                if has(i, 1, NT - 1):
                    h1_lo_part(pool, i - 1)

            pipeline(pool, step)

        @block.scalar
        def _(act):
            def hi_part(i, parity, half):
                n, full = groups_of(i, half)
                slot = 2 * parity + half
                wait(act, s_edges[slot], 16 * slot_turn(i, parity) + (16 if full < n else 0))
                wait(act, s_summed, NPARTS * (i - 2) + half + 2)
                for p, a, b in [(P, 0, full)] + ([(TAIL_P, full, n)] if full < n else []):
                    hi = act.activation(hilo[0:p, slot, a:b, :, 0, :].rearrange("p g j d -> p (g j) d"),
                                        raw[0:p, slot, a:b].rearrange("p g j d -> p (g j) d"), ACT.Copy)
                hi.then_inc(s_hi, 1)

            def clear_bank(k):
                act.activation(agg_ps[0:ED, k, :], zeros[0:ED, :].broadcast_to([ED, BANK]),
                               ACT.Copy).then_inc(s_clear, 1)

            act.wait_ge(s_pool_const, 11)
            act.activation(silu_try[:, :], zeros[:, :], ACT.Silu)
            for k in range(2):
                clear_bank(k)
            hi_part(0, 0, 0)
            for c in range(ROWS):
                n = P if c < FULL_ROWS else LAST_G
                act.wait_ge(s_relT, c + 1)
                act.activation(rel[:, c * P:c * P + n, :],
                               row_banks[c].rearrange("p (j r) -> p r j", j=PER)[:, 0:n, :],
                               ACT.Copy).then_inc(s_rel, 1)
                if c == 0:
                    hi_part(0, 0, 1)
            act.wait_ge(s_const, CONSTS)
            act.activation(w2_hi[:, :, :].rearrange("p m n -> p (m n)"), w2_in.rearrange("p m n -> p (m n)"),
                           ACT.Copy).then_inc(s_w_hi, 1)
            act.activation(w1x_hi[:, :], w1x_in, ACT.Copy).then_inc(s_w_hi, 1)
            for a in (0, ROW2):
                act.activation(w1e_hi[a:a + ED, :], w1e_in[a:a + ED, :], ACT.Copy).then_inc(s_w_hi, 1)
            def normalize(i, parity):
                np_ = nodes_p(i)
                act.wait_ge(s_x[parity], 16 * slot_turn(i, parity) + (16 if np_ != TP else 0))
                act.wait_ge(s_nmr, i + 1)
                wait(act, s_tp, i - 1)
                wait(act, s_plain, i - 1)
                for q in range(PER):
                    ln = act.activation(xn[0:np_, parity, q, :], x_t[0:np_, parity, q, :], ACT.Identity,
                                        bias=nmr[0:np_, parity, q:q + 1], scale=rstd[0:np_, parity, q:q + 1])
                ln.then_inc(s_xn, 1)

            def split_agg(t, parity):
                n = PER * nodes_p(t)
                act.wait_ge(s_agg, t + 1)
                wait(act, s_z1, M * t)
                act.activation(agg_hilo[0:ED, 0:n], agg[:, 0:n], ACT.Copy).then_inc(s_agg_hi, 1)

            def relu(t):
                np_ = nodes_p(t)
                act.wait_ge(s_tp, t + 1)
                wait(act, s_z1, M * t)
                act.activation(hT_hi[:, 0:PER * np_].rearrange("d (p q) -> d q p", q=PER),
                               tp[:, 0:PER * np_].rearrange("d (q p) -> d q p", q=PER),
                               ACT.Relu).then_inc(s_hT, 1)

            def step(i, parity):
                relu_first = isinstance(i, int) and i in (1, NT)
                if has(i, -1, NT):
                    hi_part(i + 1, 1 - parity, 0)
                if relu_first:
                    relu(i - 1)
                if has(i, 1, NT):
                    split_agg(i - 1, 1 - parity)
                if has(i, 2, NT):
                    t, n = i - 2, PER * nodes_p(i - 2)
                    for m in range(M):
                        act.wait_ge(s_z2, M * t + m + 1)
                        wait(act, s_z3, t)
                        act.activation(h2[:, m, 0:n], z[:, m, 0:n], ACT.Silu,
                                       bias=b2c[:, m:m + 1]).then_inc(s_h2, 1)
                if has(i, 1, NT - 2):
                    act.wait_ge(s_carried, i)
                    clear_bank(1 - parity)
                if has(i, 1, NT) and not relu_first:
                    relu(i - 1)
                if has(i, -1, NT):
                    hi_part(i + 1, 1 - parity, 1)
                if has(i, 0, NT):
                    normalize(i, parity)
                if has(i, 1, NT):
                    t, n = i - 1, PER * nodes_p(i - 1)
                    for m in range(M):
                        act.wait_ge(s_z1, M * t + m + 1)
                        wait(act, s_h1_lo, M * (t - 1) + m + 1)
                        act.activation(h1[:, m, 0:n], layer1_banks(t)[:, m, 0:n], ACT.Silu,
                                       bias=b1c[:, m:m + 1]).then_inc(s_h1, 1)
                        act.wait_ge(s_h1, M * t + m + 1)
                        wait(act, s_z2, M * t)
                        act.activation(h1_hi[:, m, 0:n], h1[:, m, 0:n], ACT.Copy).then_inc(s_h1_hi, 1)

            pipeline(act, step)

        @block.vector
        def _(dve):
            links = [0]

            def link(*together):
                links[0] += len(together)
                for ins in together:
                    ins.then_inc(s_idx, 1)
                dve.wait_ge(s_idx, links[0])

            to_tile = (
                lambda node: dve.tensor_scalar(g["tilet"][:, :], node[:, :], 0.5 - TILE / 2, 1.0 / TILE,
                                               ALU.add, ALU.mult),
                lambda: dve.tensor_scalar(g["tile"][:, :], g["tilet"][:, :], MAGIC, -MAGIC, ALU.add, ALU.add),
                lambda: dve.tensor_scalar(g["tile_half"][:, :], g["tile"][:, :], 0.5, -0.25, ALU.mult, ALU.add),
                lambda: dve.tensor_scalar(g["pair"][:, :], g["tile_half"][:, :], MAGIC, -MAGIC, ALU.add, ALU.add),
                lambda: dve.scalar_tensor_tensor(g["parity"][:, :], g["pair"][:, :], -2.0, g["tile"][:, :],
                                                 ALU.mult, ALU.add),
                lambda node: dve.scalar_tensor_tensor(g["offset"][:, :], g["tile"][:, :], -float(TILE), node[:, :],
                                                      ALU.mult, ALU.add),
                lambda: dve.scalar_tensor_tensor(g["offset2"][:, :], g["parity"][:, :], float(BANK), g["offset"][:, :],
                                                 ALU.mult, ALU.add))

            link(*[dve.memset(tile[:, :], 0) for tile in (g["base"], g["middle"], farthest)])
            dve.wait_ge(s_pool_const, 12)
            link(dve.tensor_scalar(window[:, :], window_i[:, :], -REACH, None, ALU.add),
                 dve.tensor_copy(g["centre"][:, :], centre_i[:, :]))
            for step_of_tile in to_tile:
                link(step_of_tile(g["centre"]) if step_of_tile in (to_tile[0], to_tile[5]) else step_of_tile())
            link(dve.tensor_copy(g["at_centre"][:, :], g["offset2"][:, :]))
            dve.wait_ge(s_dst, 64)
            row_sets = ((P, slice(0, FULL_ROWS)), (LAST_G, slice(FULL_ROWS, ROWS)))
            link(*[dve.tensor_copy(g["base"][0:r, c], dst_rows[0:r, c, 0]) for r, c in row_sets])
            link(dve.tensor_scalar(g["middle"][:, :], g["base"][:, :], REACH, None, ALU.add))
            for c in range(ROWS):
                r = P if c < FULL_ROWS else LAST_G
                dve.tensor_scalar(rel_rows[0:r, c, :], dst_rows[0:r, c, :], g["middle"][0:r, c:c + 1], None,
                                  ALU.subtract).then_inc(s_relrow, 1)
            dve.wait_ge(s_relrow, ROWS)
            for r, c in row_sets:
                last = dve.tensor_reduce(farthest[0:r, c], rel_rows[0:r, c, :], AX.X, ALU.max,
                                         apply_absolute_value=True)
            link(last)

            def load_stats(i, parity):
                np_ = nodes_p(i)
                dve.wait_ge(s_x[parity], 16 * slot_turn(i, parity) + (16 if np_ != TP else 0))
                wait(dve, s_rstd, i - 1)
                wait(dve, s_nmr, i - 1)
                for q in range(PER):
                    st = dve.bn_stats(stats[0:np_, q, :], x_t[0:np_, parity, q, :])
                st.then_inc(s_stats, 1)

            def aggregate_stats(i, parity):
                np_ = nodes_p(i)
                for q in range(PER):
                    mv = dve.bn_aggr(meanvar[0:np_, parity, q, :], stats[0:np_, q, :])
                mv.then_inc(s_mv, 1)

            def shift_of_norm(i, parity):
                np_ = nodes_p(i)
                dve.wait_ge(s_rstd, i + 1)
                wait(dve, s_xn, i - 1)
                dve.scalar_tensor_tensor(nmr[0:np_, parity], meanvar[0:np_, parity, :, 0], -1.0,
                                         rstd[0:np_, parity], ALU.mult, ALU.mult).then_inc(s_nmr, 1)

            def onehot_of(i, parity, half):
                n, _ = groups_of(i, half)
                slot = 2 * parity + half
                cols = rel[:, :, :].rearrange("p g j -> p (g j)")[
                    :, bass.ds((i * GPT + half * HALF) * PER, n * PER)]
                return dve.tensor_tensor(onehot[:, slot, 0:n * PER, :],
                                         window[:, :].unsqueeze(1).broadcast_to([P, n * PER, WINDOW]),
                                         cols.unsqueeze(2).broadcast_to([P, n * PER, WINDOW]), ALU.is_equal)

            def make_onehot(i, parity, half):
                wait(dve, s_summed, NPARTS * (i - 2) + half + 2)
                onehot_of(i, parity, half).then_inc(s_onehot, 1)

            link(dve.tensor_tensor(g["drift"][:, :], g["base"][:, :], g["centre"][:, :], ALU.subtract), to_tile[0](g["base"]))
            link(dve.tensor_scalar(g["ok1"][:, :], g["drift"][:, :], -float(SLACK), None, ALU.is_ge), to_tile[1]())
            link(dve.scalar_tensor_tensor(g["ok2"][:, :], g["drift"][:, :], float(SLACK), g["ok1"][:, :],
                                          ALU.is_le, ALU.mult), to_tile[2]())
            link(dve.scalar_tensor_tensor(g["ok3"][:, :], g["base"][:, :], 0.0, g["ok2"][:, :],
                                          ALU.is_ge, ALU.mult), to_tile[3]())
            link(dve.scalar_tensor_tensor(g["valid"][:, :], farthest[:, :], REACH, g["ok3"][:, :],
                                          ALU.is_le, ALU.mult), to_tile[4]())
            link(to_tile[5](g["base"]))
            link(dve.tensor_scalar(g["invalid"][:, :], g["valid"][:, :], -1.0, 1.0, ALU.mult, ALU.add),
                 to_tile[6]())
            link(dve.tensor_tensor(g["instead"][:, :], g["invalid"][:, :], g["at_centre"][:, :], ALU.mult),
                 dve.tensor_tensor(g["offset3"][:, :], g["offset2"][:, :], g["valid"][:, :], ALU.mult))
            dve.tensor_tensor(g["placed"][:, :], g["offset3"][:, :], g["instead"][:, :], ALU.add).then_inc(s_small, 1)
            dve.wait_ge(s_rel, 1)
            make_onehot(0, 0, 0)
            dve.wait_ge(s_smallT, 1)
            dve.tensor_copy(offset_row[:, :], z3[0:1, :, :].rearrange("p q d -> p (q d)"))
            dve.tensor_reduce(any_invalid[:, :], tp[0:1, 0:2], AX.X, ALU.max).then_inc(s_off, 1)
            make_onehot(0, 0, 1)
            dve.wait_ge(s_rel, ROWS)

            def general_path():
                chain = [0]

                def step_of(ins):
                    chain[0] += 1
                    ins.then_inc(s_gen_chain, 1)
                    dve.wait_ge(s_gen_chain, chain[0])

                def turn(rounds, into, shift, sign):
                    for c in range(ROWS):
                        r = P if c < FULL_ROWS else LAST_G
                        dve.tensor_scalar(rel_rows[0:r, c, :], dst_rows[0:r, c, :], shift[0:r, c:c + 1], None,
                                          sign).then_inc(s_gen_rows, 1)
                    dve.wait_ge(s_gen_relT, ROWS * (rounds + 1))
                    for c in range(ROWS):
                        r = P if c < FULL_ROWS else LAST_G
                        ins = dve.tensor_copy(into[:, c * P:c * P + r, :],
                                              row_banks[c].rearrange("p (j r) -> p r j", j=PER)[:, 0:r, :])
                    step_of(ins)

                dve.wait_ge(s_relT, ROWS)
                step_of(dve.tensor_scalar(g["ok1"][:, :], g["valid"][:, :], FAR, None, ALU.mult))
                step_of(dve.scalar_tensor_tensor(g["shift"][:, :], g["invalid"][:, :], FAR, g["middle"][:, :],
                                                 ALU.mult, ALU.add))
                step_of(dve.tensor_copy(tile_cols, tile_i))
                dve.wait_ge(s_carry0, 1)
                dve.wait_ge(s_carry0_dma, 32)
                turn(0, gen_rel, g["ok1"], ALU.add)
                dve.wait_ge(s_onehot, 2)
                turn(1, rel, g["shift"], ALU.subtract)
                dve.wait_ge(s_summed, 1)
                for half in range(2):
                    step_of(onehot_of(0, 0, half))
                before = chain[0]

                def group(gr):
                    dve.tensor_copy(gen_cols[:, :], gen_rel[:, bass.ds(gr, 1), :].rearrange(
                        "p g j -> p (g j)")).then_inc(s_gen_chain, 1)
                    with dve.Fori(0, NT) as n:
                        dve.wait_ge(s_gen_chain, gr * (2 * NT + 1) + 2 * n + 1 + before)
                        for j in range(PER):
                            ins = dve.tensor_scalar(gen_onehot[:, j, :], tile_cols[:, :], gen_cols[:, j:j + 1], None,
                                                    ALU.is_equal)
                        ins.then_inc(s_gen_onehot, 1)
                        dve.wait_ge(s_gen_sum, gr * NT + n + 1)
                        into = agg_carry[0:ED, bass.ds(n * TILE, TILE)]
                        dve.tensor_tensor(into, z3[0:ED, :, :].rearrange("p q d -> p (q d)")[:, 0:TILE], into,
                                          ALU.add).then_inc(s_gen_chain, 1)
                        dve.wait_ge(s_gen_onehot, gr * NT + n + 1)
                        dve.tensor_scalar(gen_cols[:, :], gen_cols[:, :], -float(TILE), None,
                                          ALU.add).then_inc(s_gen_chain, 1)
                    dve.wait_ge(s_gen_chain, gr * (2 * NT + 1) + 2 * NT + 1 + before)

                with dve.Fori(0, NG) as gr:
                    group(gr)
                dve.wait_ge(s_resummed, 1)

            where_invalid(dve, mybir.EngineType.DVE, general_path)

            def stage_sums(i, parity, s):
                a, b = part_of(i, s)
                k = (parity + s) % 2
                dve.wait_ge(s_summed, NPARTS * i + s + 1)
                wait(dve, s_placed, NPARTS * i + s - 1)
                dve.tensor_reduce(staged[0:WINDOW, k, 0:b - a, :],
                                  stage[0:WINDOW, k, 0:2 * ED * (b - a)].rearrange("w (g h d) -> w g d h", h=2, d=ED),
                                  AX.X, ALU.add).then_inc(s_staged, 1)

            def add_b3(t, parity):
                np_ = nodes_p(t)
                dve.wait_ge(s_plain, t + 1)
                if isinstance(t, int) and t == 0:
                    dve.wait_ge(s_const, CONSTS)
                dve.tensor_tensor(resid[0:np_, parity], resid[0:np_, parity],
                                  b3r[0:np_, :].unsqueeze(1).broadcast_to([np_, PER, D]),
                                  ALU.add).then_inc(s_resid, 1)

            def carry_over(t, parity):
                n = PER * nodes_p(t)
                if isinstance(t, int) and t == NT - 1:
                    dve.wait_ge(s_placed, NPARTS * NT)
                else:
                    dve.wait_ge(s_closed, t + 1)
                dve.wait_ge(s_carry0, 1)
                dve.wait_ge(s_carry0_dma, 32)
                wait(dve, s_carried, t)
                wait(dve, s_agg_lo, t)
                dve.tensor_tensor(agg[:, 0:n], agg_ps[0:ED, parity, 0:n],
                                  agg_carry[:, bass.ds(t * TILE, n)], ALU.add).then_inc(s_agg, 1)
                if has(t, 0, NT - 1):
                    over = agg_carry[:, bass.ds((t + 1) * TILE, OVER)]
                    dve.tensor_tensor(over, agg_ps[0:ED, parity, TILE:BANK], over,
                                      ALU.add).then_inc(s_carried, 1)

            def add_x(t, parity):
                np_ = nodes_p(t)
                dve.wait_ge(s_xn, t + 1)
                wait(dve, s_out, t - 1)
                dve.scalar_tensor_tensor(resid[0:np_, parity].rearrange("p q d -> p (q d)"),
                                         xn[0:np_, parity].rearrange("p q d -> p (q d)"), 0.0,
                                         x_t[0:np_, parity].rearrange("p q d -> p (q d)"),
                                         ALU.max, ALU.add).then_inc(s_plain, 1)

            def agg_lo(t):
                n = PER * nodes_p(t)
                dve.wait_ge(s_agg_hi, t + 1)
                dve.tensor_tensor(agg_hilo[ROW2:ROW2 + ED, 0:n], agg[:, 0:n], agg_hilo[0:ED, 0:n].bitcast(F32),
                                  ALU.subtract).then_inc(s_agg_lo, 1)

            def relu_lo(t):
                np_ = nodes_p(t)
                dve.wait_ge(s_hT, t + 1)
                wait(dve, s_z1, M * t)
                dve.scalar_tensor_tensor(hT_lo[:, 0:PER * np_].rearrange("d (p q) -> d q p", q=PER),
                                         tp[:, 0:PER * np_].rearrange("d (q p) -> d q p", q=PER), 0.0,
                                         hT_hi[:, 0:PER * np_].bitcast(F32).rearrange("d (p q) -> d q p", q=PER),
                                         ALU.max, ALU.subtract).then_inc(s_hT_lo, 1)

            def step(i, parity):
                early = isinstance(i, int) and i < 2
                relu_first = isinstance(i, int) and i in (1, NT)
                if has(i, 0, NT):
                    stage_sums(i, parity, 0)
                if isinstance(i, int) and i == 1:
                    dve.wait_ge(s_w_hi, 4)
                    for lo, whole, hi in (
                            (w2_lo[:, :, :].rearrange("p m n -> p (m n)"), w2_in.rearrange("p m n -> p (m n)"),
                             w2_hi[:, :, :].rearrange("p m n -> p (m n)")),
                            (w1x_lo[:, :], w1x_in, w1x_hi[:, :]),
                            (w1e_lo[:, :], w1e_in[0:ED, :], w1e_hi[0:ED, :])):
                        dve.tensor_tensor(lo, whole, hi.bitcast(F32), ALU.subtract).then_inc(s_w_lo, 1)
                if has(i, 0, NT):
                    load_stats(i, parity)
                    dve.wait_ge(s_stats, i + 1)
                    stage_sums(i, parity, 1)
                    aggregate_stats(i, parity)
                if relu_first:
                    relu_lo(i - 1)
                if has(i, 1, NT):
                    carry_over(i - 1, 1 - parity)
                    add_x(i - 1, 1 - parity)
                    agg_lo(i - 1)
                if early:
                    stage_sums(i, parity, 2)
                    make_onehot(i + 1, 1 - parity, 0)
                if has(i, 0, NT):
                    shift_of_norm(i, parity)
                if has(i, 1, NT):
                    add_b3(i - 1, 1 - parity)
                if has(i, 0, NT) and not early:
                    stage_sums(i, parity, 2)
                if has(i, 1, NT) and not relu_first:
                    relu_lo(i - 1)
                if has(i, -1, NT) and not early:
                    make_onehot(i + 1, 1 - parity, 0)
                if isinstance(i, int) and i == NT:
                    h1_lo_part(dve, i - 1)
                if has(i, 2, NT):
                    t, tp_ = i - 2, nodes_p(i - 2)
                    dve.wait_ge(s_z3, t + 1)
                    dve.wait_ge(s_resid, t + 1)
                    wait(dve, s_stored[parity], 16 * (slot_turn(t, parity) - 1))
                    dve.tensor_tensor(out_t[0:tp_, parity], z3[0:tp_, :, :], resid[0:tp_, parity],
                                      ALU.add).then_inc(s_out, 1)
                if has(i, -1, NT):
                    make_onehot(i + 1, 1 - parity, 1)

            pipeline(dve, step)

        @block.tensor
        def _(pe):
            pe.wait_ge(s_pool_const, 12)
            n_groups = [P] * FULL_ROWS + [LAST_G]
            for c, r in enumerate(n_groups):
                pe.wait_ge(s_relrow, c + 1)
                for j in range(PER):
                    tr = pe.transpose(row_banks[c][:, j * P:j * P + r],
                                      rel_rows[0:r, c, :].rearrange("r (p j) -> r j p", j=PER)[:, j, :],
                                      ident[0:r, 0:r])
                tr.then_inc(s_relT, 1)

            def one_hot_sums(i, parity, s):
                a, b = part_of(i, s)
                bank = (parity + s) % 2
                for k in range(a, b):
                    half = k // HALF
                    full = groups_of(i, half)[1]
                    rows = P if k - half * HALF < full else TAIL_P
                    slot = 2 * parity + half
                    if k == a or k == HALF:
                        pe.wait_ge(s_lo, 2 * i + half + 1)
                        pe.wait_ge(s_onehot, 2 * i + half + 1)
                    for j in range(PER):
                        c = 2 * ED * (k - a)
                        mm = pe.matmul(stage[0:WINDOW, bank, c:c + 2 * ED],
                                       onehot[0:rows, slot, (k - half * HALF) * PER + j, :],
                                       hilo[0:rows, slot, k - half * HALF, j].rearrange("p h d -> p (h d)"),
                                       start=(k == a and j == 0), stop=True, skip_group_check=True)
                return mm

            def sum_groups(i, parity, s):
                one_hot_sums(i, parity, s).then_inc(s_summed, 1)

            pe.wait_ge(s_small, 1)
            pe.wait_ge(s_rel, ROWS)
            for c in range(ROWS):
                pe.matmul(z3[0:1, c, :], g["placed"][:, c:c + 1], ident[:, :], start=True, stop=True)
            for c in range(FULL_ROWS):
                pe.matmul(tp[0:1, 0:1], g["invalid"][:, c:c + 1], one[:, :],
                          start=(c == 0), stop=(c == FULL_ROWS - 1))
            pe.matmul(tp[0:1, 1:2], g["invalid"][0:LAST_G, FULL_ROWS:ROWS], one[0:LAST_G, :],
                      start=True, stop=True, skip_group_check=True).then_inc(s_smallT, 1)
            sum_groups(0, 0, 0)

            def general_path():
                for rounds in range(2):
                    for c, r in enumerate(n_groups):
                        pe.wait_ge(s_gen_rows, ROWS * rounds + c + 1)
                        for j in range(PER):
                            tr = pe.transpose(row_banks[c][:, j * P:j * P + r],
                                              rel_rows[0:r, c, :].rearrange("r (p j) -> r j p", j=PER)[:, j, :],
                                              ident[0:r, 0:r])
                        tr.then_inc(s_gen_relT, 1)
                pe.wait_ge(s_gen_chain, 7)
                one_hot_sums(0, 0, 0).then_inc(s_resummed, 1)

                def group(gr, rows):
                    with pe.Fori(0, NT) as n:
                        pe.wait_ge(s_gen_raw, (gr + 1) * 16)
                        pe.wait_ge(s_gen_onehot, gr * NT + n + 1)
                        for j in range(PER):
                            mm = pe.matmul(z3[0:ED, :, :].rearrange("p q d -> p (q d)")[:, 0:TILE],
                                           gen_raw[0:rows, j, :], gen_onehot[0:rows, j, :].bitcast(F32),
                                           start=(j == 0), stop=(j == PER - 1))
                        mm.then_inc(s_gen_sum, 1)

                with pe.Fori(0, NG - 1) as gr:
                    group(gr, P)
                group(NG - 1, TAIL_P)

            where_invalid(pe, mybir.EngineType.PE, general_path)
            banks = agg_ps[:, :, :].rearrange("p k n -> p (k n)")
            pe.wait_ge(s_clear, 2)

            def place_groups(i, parity, s, offsets):
                a, b = part_of(i, s)
                pe.wait_ge(s_staged, NPARTS * i + s + 1)
                for k in range(a, b):
                    if k == GPT - EARLY and has(i, -1, NT):
                        pe.wait_ge(s_clear, i + 2)
                    mm = pe.matmul(banks[0:ED, bass.ds(offsets[k - a], WINDOW)],
                                   staged[:, (parity + s) % 2, k - a, :], ident[0:PLACE_K, 0:WINDOW],
                                   start=False, stop=True, skip_group_check=True)
                    if k == EARLY - 1 and has(i, 1, NT):
                        mm.then_inc(s_closed, 1)
                mm.then_inc(s_placed, 1)

            def transposes(i, parity):
                t, np_ = i - 1, nodes_p(i - 1)
                if isinstance(i, int) and i in (1, NT):
                    pe.wait_ge(s_xn, t + 1)
                if not has(i, 0, NT):
                    wait(pe, s_hT_lo, t)
                for q in range(PER):
                    tr = pe.transpose(tp[:, q * np_:(q + 1) * np_], xn[0:np_, 1 - parity, q, :],
                                      ident[0:np_, 0:np_])
                tr.then_inc(s_tp, 1)

            def layer2(i, parity):
                t, n = i - 2, PER * nodes_p(i - 2)
                pe.wait_ge(s_h1_hi, M * t + M)
                for k in range(M):
                    for m in range(M):
                        pe.matmul(z[:, m, 0:n], w2_hi[:, k, m * P:(m + 1) * P], h1_hi[:, k, 0:n],
                                  start=(k == 0), stop=False)
                        pe.matmul(z[:, m, 0:n], w2_lo[:, k, m * P:(m + 1) * P], h1_hi[:, k, 0:n],
                                  start=False, stop=False)
                for m in range(M):
                    for k in range(M):
                        if m == 0:
                            pe.wait_ge(s_h1_lo, M * t + k + 1)
                        mm = pe.matmul(z[:, m, 0:n], w2_hi[:, k, m * P:(m + 1) * P], h1_lo[:, k, 0:n],
                                       start=False, stop=(k == M - 1))
                    mm.then_inc(s_z2, 1)

            def layer3(i, parity):
                t, np_ = i - 2, nodes_p(i - 2)
                if not has(i, 0, NT):
                    wait(pe, s_out, t)
                pe.wait_ge(s_h2, M * t + M)
                for q in range(PER):
                    for k in range(M):
                        mm = pe.matmul(z3[0:np_, q, :],
                                       h2[:, k, 0:PER * np_].rearrange("c (p q) -> c q p", q=PER)[:, q, :],
                                       w3[:, k, :], start=(k == 0), stop=(k == M - 1))
                mm.then_inc(s_z3, 1)

            def layer1(i, parity):
                t, n = i - 1, PER * nodes_p(i - 1)
                sums = layer1_banks(t)
                pe.wait_ge(s_hT_lo, t + 1)
                if isinstance(t, int) and t == 0:
                    pe.wait_ge(s_w_lo, 3)
                    pe.wait_ge(s_w_hi, 4)
                    pe.wait_ge(s_const, CONSTS)
                for m in range(M):
                    for w, act_ in ((w1x_hi, hT_hi), (w1x_lo, hT_hi), (w1x_hi, hT_lo)):
                        pe.matmul(sums[:, m, 0:n], w[:, m * P:(m + 1) * P], act_[:, 0:n],
                                  start=(w is w1x_hi and act_ is hT_hi), stop=False)
                    if isinstance(i, int) and i in (1, NT):
                        pe.wait_ge(s_agg_lo, t + 1)
                    pe.matmul(sums[:, m, 0:n], w1e_hi[:, m * P:(m + 1) * P], agg_hilo[:, 0:n],
                              start=False, stop=False)
                    pe.matmul(sums[:, m, 0:n], w1e_lo[:, m * P:(m + 1) * P], agg_hilo[0:ED, 0:n],
                              start=False, stop=True).then_inc(s_z1, 1)

            def step(i, parity):
                before = part_of(i - 1, 2)[1] - PARTS[2][0] if has(i, 1, NT) else 0
                first_group = i * GPT - before if isinstance(i, int) and i < NT else i * GPT - (GPT - PARTS[2][0])
                count = before + (PARTS[1][1] if has(i, 0, NT) else 0)
                if count:
                    _, offs = nc.values_load_multi_w_load_instructions(
                        offset_row[0:1, bass.ds(first_group, count)], engines=[mybir.EngineType.PE],
                        min_val=0, max_val=2 * BANK - WINDOW,
                        skip_runtime_bounds_check_because="valid groups lie within SLACK of their tile")
                if has(i, 0, NT) and not (isinstance(i, int) and i == 0):
                    sum_groups(i, parity, 0)
                if has(i, 1, NT):
                    place_groups(i - 1, 1 - parity, 2, offs[:before])
                if has(i, 0, NT):
                    sum_groups(i, parity, 1)
                    place_groups(i, parity, 0, offs[before:])
                if isinstance(i, int) and i == NT:
                    transposes(i, parity)
                    layer2(i, parity)
                    layer1(i, parity)
                    layer3(i, parity)
                    return
                if has(i, 2, NT):
                    layer2(i, parity)
                if has(i, 1, NT):
                    transposes(i, parity)
                if has(i, 0, NT):
                    sum_groups(i, parity, 2)
                    place_groups(i, parity, 1, offs[before + PARTS[0][1]:])
                if has(i, 2, NT):
                    layer3(i, parity)
                if has(i, 1, NT):
                    layer1(i, parity)

            pipeline(pe, step)


_INS = ["x", "dst", "edge_attr_48", "L0_gnn_W1", "L0_gnn_b1", "L0_gnn_W2", "L0_gnn_b2", "L0_gnn_W3", "L0_gnn_b3"]


def kernel(**inputs):
    import numpy as _np
    import concourse.bacc as _bacc
    from concourse import mybir as _mybir
    from concourse.bass_utils import run_bass_kernel_spmd as _run

    nc = _bacc.Bacc("TRN2", target_bir_lowering=False, num_devices=1)
    arrays, args = {}, []
    for name in _INS:
        a = _np.ascontiguousarray(inputs[name])
        arrays[f"in_{name}_dram"] = a
        args.append(nc.dram_tensor(f"in_{name}_dram", a.shape, _mybir.dt.from_np(a.dtype), kind="ExternalInput").ap())
    out = nc.dram_tensor("out_0_dram", inputs["x"].shape, _mybir.dt.float32, kind="ExternalOutput").ap()
    gnn_kernel(nc, *args, out)
    r = _run(nc, [arrays], core_ids=[0])
    return r.results[0]["out_0_dram"]
```
